# Optimizing a Trainium2 kernel written in Bass

```python
import numpy as np
import jax
import jax.numpy as jnp

def _softmax(x, axis=-1):
    return jax.nn.softmax(x, axis=axis)

def _gelu(x):
    return jax.nn.gelu(x, approximate=True)

def _silu(x):
    return jax.nn.silu(x)

def _sigmoid(x):
    return jax.nn.sigmoid(x)

def _layernorm(x, axis=-1, eps=1e-05):
    m = jnp.mean(x, axis=axis, keepdims=True)
    v = jnp.var(x, axis=axis, keepdims=True)
    return (x - m) / jnp.sqrt(v + eps)

def _scatter_add(tgt, idx, src, axis=0):
    return tgt.at[idx].add(src)

def _segment_sum(src, seg, n):
    return jax.ops.segment_sum(src, seg, n)
kernel_name = 'mk_xattn_seq_d2_seqx_r4_04096b'

def setup_inputs(seed: int=0):
    np.random.seed(seed)
    _w = jnp.asarray

    def _rec_inputs():
        import jax
        import jax.numpy as jnp
        _rk = jax.random.key(seed)
        x = -0.0001108 + 0.9999 * jax.random.normal(jax.random.fold_in(_rk, 1), (32, 112, 320), jnp.float32)
        _lenS = 112 - jax.random.randint(jax.random.fold_in(_rk, 7), (32,), 0, max(1, 112 // 4) + 1, jnp.int32)
        _lenS2 = 375 - jax.random.randint(jax.random.fold_in(_rk, 8), (32,), 0, max(1, 375 // 4) + 1, jnp.int32)
        _ctx_2048P = jax.random.normal(jax.random.fold_in(_rk, 11), (32, 16, 512), jnp.float32)
        _ctx_2048c = jax.random.dirichlet(jax.random.fold_in(_rk, 511), 0.3 * jnp.ones((16,), jnp.float32), (32, 375))
        _ctx_2048t = jnp.einsum('bsk,bkd->bsd', _ctx_2048c, _ctx_2048P)
        _ctx_2048t = _ctx_2048t * jax.lax.rsqrt(jnp.mean(jnp.square(_ctx_2048t)) + 1e-12) * 0.953939
        ctx_2048 = -0.000395056 + 1.00006 * (_ctx_2048t + 0.3 * jax.random.normal(jax.random.fold_in(_rk, 611), (32, 375, 512), jnp.float32))
        fside_S_0 = jax.random.uniform(jax.random.fold_in(_rk, 12), (112,), jnp.float32, 0.0, 0.999706)
        return (x, ctx_2048, fside_S_0)
    x, ctx_2048, fside_S_0 = _rec_inputs()

    def _L0_xattn_setup():
        import jax, jax.numpy as jnp
        import numpy as np
        NUM_HEADS = 20
        TEXT_LEN = 77
        IP_SCALE = 1.0

        def _attend(q, k, v, sm_scale):
            scores = jnp.einsum('bhsd,bhld->bhsl', q, k) * sm_scale
            probs = jax.nn.softmax(scores, axis=-1)
            return jnp.einsum('bhsl,bhld->bhsd', probs, v)

        def _split_heads(x, h):
            b, s, c = x.shape
            return x.reshape(b, s, h, c // h).transpose(0, 2, 1, 3)

        def _merge_heads(x):
            b, h, s, d = x.shape
            return x.transpose(0, 2, 1, 3).reshape(b, s, h * d)
        key = jax.random.key(seed)
        ks = jax.random.split(key, 8)
        B, S, C, CC, L = (8, 1024, 320, 512, TEXT_LEN + 4)
        sd_q = 1.0 / np.sqrt(C)
        sd_kv = 1.0 / np.sqrt(CC)
        return {'hidden_states': jax.random.normal(ks[0], (B, S, C), jnp.float32), 'encoder_hidden_states': jax.random.normal(ks[1], (B, L, CC), jnp.float32), 'Wq': jax.random.normal(ks[2], (C, C), jnp.float32) * sd_q, 'Wk': jax.random.normal(ks[3], (C, CC), jnp.float32) * sd_kv, 'Wv': jax.random.normal(ks[4], (C, CC), jnp.float32) * sd_kv, 'Wk_ip': jax.random.normal(ks[5], (C, CC), jnp.float32) * sd_kv, 'Wv_ip': jax.random.normal(ks[6], (C, CC), jnp.float32) * sd_kv, 'Wo': jax.random.normal(ks[7], (C, C), jnp.float32) * sd_q, 'bo': jnp.zeros((C,), jnp.float32)}
    _L0_xattn_all = _L0_xattn_setup()
    _L0_xattn_in = {k: v for k, v in _L0_xattn_all.items() if k in ('Wq', 'Wk', 'Wv', 'Wk_ip', 'Wv_ip', 'Wo', 'bo')}
    del _L0_xattn_all

    def _L1_xattn_setup():
        import jax, jax.numpy as jnp
        import numpy as np
        HEADS = 20
        NUM_TOKENS = 4
        IP_SCALE = 1.0
        SEM_SCALE = 0.5
        RESCALE = 1.0
        EPS = 1e-12

        def _l2norm(x, axis=-1):
            n = jnp.sqrt(jnp.sum(x * x, axis=axis, keepdims=True))
            return x / jnp.maximum(n, EPS)
        key = jax.random.key(seed)
        ks = jax.random.split(key, 10)
        B, S, C = (2, 256, 320)
        T, E = (81, 512)
        inp = {'hidden_states': jax.random.normal(ks[0], (B, S, C), jnp.float32), 'encoder_hidden_states': jax.random.normal(ks[1], (B, T, E), jnp.float32), 'spatial_mask': jax.random.uniform(ks[2], (S,), jnp.float32), 'W_q': jax.random.normal(ks[3], (C, C), jnp.float32) * C ** (-0.5), 'W_k': jax.random.normal(ks[4], (E, C), jnp.float32) * E ** (-0.5), 'W_v': jax.random.normal(ks[5], (E, C), jnp.float32) * E ** (-0.5), 'W_k_ip': jax.random.normal(ks[6], (E, C), jnp.float32) * E ** (-0.5), 'W_v_ip': jax.random.normal(ks[7], (E, C), jnp.float32) * E ** (-0.5), 'W_out': jax.random.normal(ks[8], (C, C), jnp.float32) * C ** (-0.5), 'b_out': jnp.zeros((C,), jnp.float32)}
        return inp
    _L1_xattn_all = _L1_xattn_setup()
    _L1_xattn_in = {k: v for k, v in _L1_xattn_all.items() if k in ('W_q', 'W_k', 'W_v', 'W_k_ip', 'W_v_ip', 'W_out', 'b_out')}
    del _L1_xattn_all
    return {'x': x, 'ctx_2048': ctx_2048, 'fside_S_0': fside_S_0, 'L0_xattn_Wq': _L0_xattn_in['Wq'], 'L0_xattn_Wk': _L0_xattn_in['Wk'], 'L0_xattn_Wv': _L0_xattn_in['Wv'], 'L0_xattn_Wk_ip': _L0_xattn_in['Wk_ip'], 'L0_xattn_Wv_ip': _L0_xattn_in['Wv_ip'], 'L0_xattn_Wo': _L0_xattn_in['Wo'], 'L0_xattn_bo': _L0_xattn_in['bo'], 'L1_xattn_W_q': _L1_xattn_in['W_q'], 'L1_xattn_W_k': _L1_xattn_in['W_k'], 'L1_xattn_W_v': _L1_xattn_in['W_v'], 'L1_xattn_W_k_ip': _L1_xattn_in['W_k_ip'], 'L1_xattn_W_v_ip': _L1_xattn_in['W_v_ip'], 'L1_xattn_W_out': _L1_xattn_in['W_out'], 'L1_xattn_b_out': _L1_xattn_in['b_out']}

def reference(x, ctx_2048, fside_S_0, L0_xattn_Wq, L0_xattn_Wk, L0_xattn_Wv, L0_xattn_Wk_ip, L0_xattn_Wv_ip, L0_xattn_Wo, L0_xattn_bo, L1_xattn_W_q, L1_xattn_W_k, L1_xattn_W_v, L1_xattn_W_k_ip, L1_xattn_W_v_ip, L1_xattn_W_out, L1_xattn_b_out):
    import jax
    import jax.numpy as jnp

    def _L0_xattn_ref(hidden_states, encoder_hidden_states, Wq, Wk, Wv, Wk_ip, Wv_ip, Wo, bo):
        import jax, jax.numpy as jnp
        import numpy as np
        NUM_HEADS = 20
        TEXT_LEN = 77
        IP_SCALE = 1.0

        def _attend(q, k, v, sm_scale):
            scores = jnp.einsum('bhsd,bhld->bhsl', q, k) * sm_scale
            probs = jax.nn.softmax(scores, axis=-1)
            return jnp.einsum('bhsl,bhld->bhsd', probs, v)

        def _split_heads(x, h):
            b, s, c = x.shape
            return x.reshape(b, s, h, c // h).transpose(0, 2, 1, 3)

        def _merge_heads(x):
            b, h, s, d = x.shape
            return x.transpose(0, 2, 1, 3).reshape(b, s, h * d)
        residual = hidden_states
        B, S, C = hidden_states.shape
        H = NUM_HEADS
        D = C // H
        sm_scale = 1.0 / jnp.sqrt(jnp.asarray(D, hidden_states.dtype))
        text = encoder_hidden_states[:, :TEXT_LEN, :]
        ip = encoder_hidden_states[:, TEXT_LEN:, :]
        q = _split_heads(hidden_states @ Wq.T, H)
        k = _split_heads(text @ Wk.T, H)
        v = _split_heads(text @ Wv.T, H)
        out_text = _merge_heads(_attend(q, k, v, sm_scale))
        k_ip = _split_heads(ip @ Wk_ip.T, H)
        v_ip = _split_heads(ip @ Wv_ip.T, H)
        out_ip = _merge_heads(_attend(q, k_ip, v_ip, sm_scale))
        out = out_text + IP_SCALE * out_ip
        out = out @ Wo.T + bo
        return out + residual

    def _L1_xattn_ref(hidden_states, encoder_hidden_states, spatial_mask, W_q, W_k, W_v, W_k_ip, W_v_ip, W_out, b_out):
        import jax, jax.numpy as jnp
        import numpy as np
        HEADS = 20
        NUM_TOKENS = 4
        IP_SCALE = 1.0
        SEM_SCALE = 0.5
        RESCALE = 1.0
        EPS = 1e-12

        def _l2norm(x, axis=-1):
            n = jnp.sqrt(jnp.sum(x * x, axis=axis, keepdims=True))
            return x / jnp.maximum(n, EPS)
        B, S, C = hidden_states.shape
        H = HEADS
        Dh = C // H
        attn_scale = Dh ** (-0.5)
        residual = hidden_states
        text_ehs = encoder_hidden_states[:, :-NUM_TOKENS]
        ip_ehs = encoder_hidden_states[:, -NUM_TOKENS:]

        def heads(x):
            return x.reshape(B, -1, H, Dh).transpose(0, 2, 1, 3)
        q = heads(hidden_states @ W_q)
        k_t = heads(text_ehs @ W_k)
        v_t = heads(text_ehs @ W_v)
        scores_t = jnp.einsum('bhsd,bhtd->bhst', q, k_t) * attn_scale
        probs_t = jax.nn.softmax(scores_t, axis=-1)
        text_out = jnp.einsum('bhst,bhtd->bhsd', probs_t, v_t)
        text_out = text_out.transpose(0, 2, 1, 3).reshape(B, S, C)
        k_ip = heads(ip_ehs @ W_k_ip)
        v_ip = heads(ip_ehs @ W_v_ip)
        attn_scores = jnp.einsum('bhsd,bhnd->bhsn', q, k_ip) * attn_scale
        qsem = jnp.einsum('bhst,bte->bhse', probs_t, text_ehs)
        qsem = _l2norm(qsem)
        ip_n = _l2norm(ip_ehs)
        sem = jnp.einsum('bhse,bne->bhsn', qsem, ip_n)
        sem = jax.lax.stop_gradient(sem)
        fused = attn_scores + SEM_SCALE * sem
        probs_ip = jax.nn.softmax(fused, axis=-1)
        probs_ip = probs_ip * spatial_mask[None, None, :, None]
        ip_out = jnp.einsum('bhsn,bhnd->bhsd', probs_ip, v_ip)
        ip_out = ip_out.transpose(0, 2, 1, 3).reshape(B, S, C)
        out = text_out + IP_SCALE * ip_out
        out = out @ W_out + b_out
        out = out + residual
        return out / RESCALE
    x = _L0_xattn_ref(x, ctx_2048, L0_xattn_Wq, L0_xattn_Wk, L0_xattn_Wv, L0_xattn_Wk_ip, L0_xattn_Wv_ip, L0_xattn_Wo, L0_xattn_bo)
    x = _L1_xattn_ref(x, ctx_2048, fside_S_0, L1_xattn_W_q, L1_xattn_W_k, L1_xattn_W_v, L1_xattn_W_k_ip, L1_xattn_W_v_ip, L1_xattn_W_out, L1_xattn_b_out)
    return x

_drawn_inputs = setup_inputs


def setup_inputs(seed=0):
    import zlib

    import numpy as np

    out = dict(_drawn_inputs(seed))
    spreads = {'L0_xattn_bo': (0.0, 0.1), 'L1_xattn_b_out': (0.0, 0.1)}
    factors = {}
    for name, (base, spread) in spreads.items():
        noise = np.random.default_rng([zlib.crc32(name.encode()), seed]).standard_normal(out[name].shape)
        drawn = base * np.exp(spread * noise) if base else spread * noise
        out[name] = jnp.asarray(drawn.astype(out[name].dtype))
    for name, factor in factors.items():
        out[name] = (out[name] * factor).astype(out[name].dtype)
    return out
```

```python
from contextlib import ExitStack

import concourse.bass as bass
from concourse import mybir
from concourse.alu_op_type import AluOpType as ALU

B, S, C, T, E = 32, 112, 320, 375, 512
H, D = 20, 16
TEXT0, TEXT1, NIP = 77, 371, 4
KW = 384
GH, NG = 4, 5
QW = GH * S
PADQ = 128 - S
ROWS = [128, 128, 115]
EPS2 = 1e-24
LOG_P = 8.317766166719343
QPART = [0, 1, 2, 0, 1, 0]
KPART = [0, 0, 0, 1, 1, 2]
CT = [(0, 128), (128, 128), (256, 64)]
HALVES = [(0, 12), (12, 20)]
MT = [(0, 0), (128, 0), (192, 64)]


class Queue:

    def __init__(self, sem):
        self.sem, self.n, self.steps, self.reached = sem, 0, [], {}

    def wait(self, *tokens):
        for t in tokens:
            if t is None:
                continue
            sem, value = t
            if self.reached.get(id(sem), 0) < value:
                self.reached[id(sem)] = value
                self.steps.append(lambda e, s=sem, v=value: e.wait_ge(s, v))

    def do(self, f, signal=True):
        if not signal:
            self.steps.append(f)
            return None
        self.n += 1
        self.steps.append(lambda e: f(e).then_inc(self.sem, 1))
        return self.sem, self.n

    def run(self, engine):
        for s in self.steps:
            s(engine)


class Stream:

    def __init__(self, queue, sem):
        self.queue, self.sem, self.n = queue, sem, 0

    def go(self, dst, src):
        self.n += 16
        self.queue.steps.append(lambda e: e.dma_start(dst, src).then_inc(self.sem, 16))
        return self.sem, self.n


def xattn_two_layers(nc, a, out):
    fp32, f32r, bf16, fp16 = mybir.dt.float32, mybir.dt.float32r, mybir.dt.bfloat16, mybir.dt.float16
    ACT, X = mybir.ActivationFunctionType, mybir.AxisListType.X
    ctx = ExitStack()
    with ctx:
        def sb(name, shape, dt=fp32):
            return ctx.enter_context(nc.sbuf_tensor(name, shape, dt))

        def pb(name, shape, dt=fp32):
            return ctx.enter_context(nc.psum_tensor(name, shape, dt))

        def sem(name):
            return ctx.enter_context(nc.semaphore(name))

        kd = [nc.dram_tensor(f"k_split{l}", [B, 3, C, T], bf16, kind="Internal").ap() for l in range(2)]
        qd = [nc.dram_tensor(f"q_split{l}", [B, 3, C, S], bf16, kind="Internal").ap() for l in range(2)]
        vipd = nc.dram_tensor("v_ip", [B * NIP, C], fp32, kind="Internal").ap()

        cT = [sb(f"cT{i}", [128, 4, T + 1]) for i in range(2)]
        wk = [sb(f"wk{i}", [128, 4, C]) for i in range(3)]
        wv = [sb(f"wv{i}", [128, 4, C]) for i in range(3)]
        wq = [sb(f"wq{i}", [128, 3, C]) for i in range(2)]
        wo = [sb(f"wo{i}", [128, 3, C]) for i in range(2)]
        Ks = [sb(f"Ks{i}", [102, H, KW], bf16) for i in range(2)]
        Qs = [sb(f"Qs{i}", [102, H, S], bf16) for i in range(2)]
        kst = [sb(f"kst{i}", [128, 3, T], bf16) for i in range(2)]
        rem = [sb(f"rem{i}", [128, T]) for i in range(2)]
        qst = sb("qst", [128, 3, 3, S], bf16)
        qrem = sb("qrem", [128, 3, S])
        V0t = sb("V0t", [TEXT0, H, 49], bf16)
        V0 = sb("V0", [128, 3, H, 49], bf16)
        V1 = [sb(f"V1{i}", [128, 3, H, 61], bf16) for i in range(2)]
        g4 = sb("g4", [128, 3, NIP])
        g4r = sb("g4r", [128, 3, NIP])
        g4s = sb("g4s", [128, 3, 3, NIP], bf16)
        GO = [0, T - NIP, T - NIP + 243]
        Gh = [sb(f"Gh{i}", [128, 729], f32r) for i in range(2)]
        Gl = [sb(f"Gl{i}", [128, 729], f32r) for i in range(2)]
        p32 = [sb(f"p32_{i}", [128, 3 * QW]) for i in range(2)]
        ph = [sb(f"ph_{i}", [128, 3 * QW + PADQ], fp16) for i in range(2)]
        pl = [sb(f"pl_{i}", [128, 3 * QW + PADQ], fp16) for i in range(2)]
        pr = sb("pr", [128, 3 * QW], f32r)
        w2 = [sb(f"w2_{i}", [128, 3 * QW]) for i in range(2)]
        xn = [sb(f"xn{i}", [S, C]) for i in range(2)]
        xT = [sb(f"xT{i}", [128, 3, 128]) for i in range(2)]
        x1 = [sb(f"x1_{i}", [S, C]) for i in range(2)]
        x1T = sb("x1T", [128, 3, 128])
        oT = [sb(f"oT{i}", [128, 3, S]) for i in range(2)]
        o0 = sb("o0", [S, C])
        o1 = sb("o1", [S, C])
        t1 = sb("t1", [S, C])
        acc = [sb(f"acc{i}", [S, 2 * GH, D]) for i in range(2)]
        rz = sb("rz", [S, 2 * GH])
        m0 = sb("m0", [S, 2 * H])
        m1 = sb("m1", [S, H])
        mn = sb("mn", [S, 2 * H])
        mrem = sb("mrem", [2 * H, S])
        ms = sb("ms", [2 * H, 3, S], bf16)
        sip = [sb(f"sip{i}", [S, H, NIP]) for i in range(2)]
        num = sb("num", [S, H, NIP])
        zs = sb("zs", [S, H])
        zq = sb("zq", [S, H])
        nss = sb("nss", [96, QW])
        d2 = sb("d2", [S, H])
        fus = [sb(f"fus{i}", [S, H, NIP]) for i in range(2)]
        sm = [sb(f"sm{i}", [S, H]) for i in range(3)]
        prT = sb("prT", [H * NIP, S])
        vbd = sb("vbd", [H * NIP, C])
        NI = B * NIP
        kip = sb("kip", [128, 3, 3, NI], bf16)
        ninv = sb("ninv", [128, B, NIP])
        bias = [sb(f"bias{i}", [S, C]) for i in range(2)]
        side = sb("side", [S, 1])
        ident = sb("ident_sb", [128, 128])
        sel = sb("sel_sb", [128, NG, 32])
        sel2 = sb("sel2_sb", [96, 8])
        mip = sb("mip_sb", [128, 1])
        bmask = sb("bmask_sb", [H * NIP, C], bf16)
        wkip = p32[0][:, 0:4 * C].rearrange("p (k c) -> p k c", k=4)
        wvip = p32[1][:, 0:4 * C].rearrange("p (k c) -> p k c", k=4)
        cip = w2[0][:, 0:4 * NI].rearrange("p (k c) -> p k c", k=4)
        csq = w2[1][:, 0:4 * NI].rearrange("p (k c) -> p k c", k=4)
        vipf = w2[1][:, 512:512 + C]
        ones = w2[1][:, 896:1024]

        ST = pb("ST", [128, 3, 512])
        PN = pb("PN", [128, 2, 512])
        PV, NS = PN[:, 0, :], PN[:, 1, :]
        R = [pb(f"R{i}", [128, 512]) for i in range(3)]

        pe, dve, act, pool, sp = (Queue(sem(n)) for n in ("s_pe", "s_dve", "s_act", "s_pool", "s_sp"))
        d_const = Stream(sp, sem("d_const"))
        d_ctx = [Stream(sp, sem(f"d_ctx{i}")) for i in range(2)]
        d_x = [Stream(sp, sem(f"d_x{i}")) for i in range(2)]
        d_kw = [[Stream(sp, sem(f"d_kw{l}{i}")) for i in range(2)] for l in range(2)]
        d_kr = [[Stream(sp, sem(f"d_kr{l}{i}")) for i in range(2)] for l in range(2)]
        d_qw = [Stream(sp, sem(f"d_qw{i}")) for i in range(2)]
        d_qr = [Stream(sp, sem(f"d_qr{i}")) for i in range(2)]
        d_m = [Stream(sp, sem(f"d_m{i}")) for i in range(2)]
        d_vw = Stream(sp, sem("d_vw"))
        d_v = Stream(sp, sem("d_v"))
        d_out = [Stream(sp, sem(f"d_out{i}")) for i in range(2)]

        tk = {}
        bank_free = [None, None, None]
        bank_at = [0]

        def bank():
            i = bank_at[0] % 3
            bank_at[0] += 1
            pe.wait(bank_free[i])
            return i

        def mm(o, l, r, start, stop, signal=False, shared=False):
            return pe.do(lambda e: e.matmul(o, l, r, start=start, stop=stop, skip_group_check=shared), signal)

        def transpose(o, i, idn, signal=False):
            return pe.do(lambda e: e.transpose(o, i, idn), signal)

        def vcopy(o, i):
            return dve.do(lambda e: e.tensor_copy(o, i))

        def acopy(o, i, scale=1.0):
            return act.do(lambda e: e.activation(o, i, ACT.Copy, scale=scale))

        def tt(q, o, x, y, op):
            return q.do(lambda e: e.tensor_tensor(o, x, y, op))

        def stt(o, x, s, y, op0, op1):
            return dve.do(lambda e: e.scalar_tensor_tensor(out=o, in0=x, scalar=s, in1=y, op0=op0, op1=op1))

        for dst, src in ((ident, "ident"), (sel, "sel"), (sel2, "sel2"), (mip, "mip"), (bmask, "bmask"), (side, "side")):
            tk["const"] = d_const.go(dst[:], a[src])
        for i, n in enumerate(("wk0", "wkip0", "wk1")):
            tk["const"] = d_const.go(wk[i][:], a[n].rearrange("(k e) c -> e k c", e=128))
        for i, n in enumerate(("wv0", "wvip0", "wv1")):
            tk["const"] = d_const.go(wv[i][:], a[n].rearrange("(k e) c -> e k c", e=128))
        for t_, n in ((wq[0], "wq0"), (wo[0], "wo0"), (wq[1], "wq1"), (wo[1], "wo1")):
            for k, (c0, n_) in enumerate(CT):
                tk["const"] = d_const.go(t_[0:n_, k, :], a[n][c0:c0 + n_, :])
        tk["const"] = d_const.go(wkip, a["wkip1"].rearrange("(k e) c -> e k c", e=128))
        tk["const"] = d_const.go(wvip, a["wvip1"].rearrange("(k e) c -> e k c", e=128))
        tk["const"] = d_const.go(cip, a["cip"].rearrange("(k e) c -> e k c", e=128))
        for i, n in enumerate(("bo0", "bo1")):
            tk["const"] = d_const.go(bias[i][:], a[n].rearrange("(a n) -> a n", a=1).to_broadcast([S, C]))
        clear = None
        for l in range(2):
            clear = pool.do(lambda e, t_=Ks[l]: e.memset(t_[:, :, 360:KW], 0.0))
        sp.wait(clear)
        tk["const"] = d_const.go(Qs[1][99:100, :, :], a["qone"].rearrange("(a h) q -> a h q", a=1))
        for h in range(H):
            tk["const"] = d_const.go(Ks[0][96:102, h, :], a["kones0"])
            tk["const"] = d_const.go(Ks[1][96:100, h, :], a["kones1"])
        tk["v_ones"] = pool.do(lambda e: e.memset(V0t[:, :, 48:49], 1.0))
        tk["v_ones"] = pool.do(lambda e: e.memset(V0[:, 1:3, :, 48:49], 1.0))
        for i in range(2):
            tk["v_ones"] = pool.do(lambda e, t_=V1[i]: e.memset(t_[:, :, :, 48:49], 1.0))
            for t_ in (ph[i], pl[i]):
                tk["v_ones"] = pool.do(lambda e, t_=t_: e.memset(t_[:, :], 0.0))
        tk["v_ones"] = pool.do(lambda e: e.memset(g4[:], 0.0))
        tk["v_ones"] = pool.do(lambda e: e.memset(x1T[:], 0.0))
        dve.wait(tk["const"], tk["v_ones"])
        tk["v_mask"] = vcopy(V0[:, 0, :, 48:49], mip[:].unsqueeze(1).to_broadcast([128, H, 1]))
        t = dve.do(lambda e: e.memset(ones, 1.0))
        tsq = tt(dve, csq, cip, cip, ALU.mult)
        for e_ in (pe, act, pool):
            e_.wait(tk["const"], tk["v_mask"])
        for m, (c0, _) in enumerate(MT):
            i = bank()
            for k in range(4):
                done = mm(R[i][:, 0:NI], wkip[:, k, c0:c0 + 128], cip[:, k, :], k == 0, k == 3, k == 3)
            act.wait(done)
            hi = acopy(kip[:, m, 0, :], R[i][:, 0:NI])
            dve.wait(hi)
            r = tt(dve, rem[0][:, 0:NI], R[i][:, 0:NI], kip[:, m, 0, :], ALU.subtract)
            bank_free[i] = r
            dve.wait(r)
            mid = vcopy(kip[:, m, 1, :], rem[0][:, 0:NI])
            dve.wait(mid)
            tk["kip"] = tt(dve, kip[:, m, 2, :], rem[0][:, 0:NI], kip[:, m, 1, :], ALU.subtract)
            dve.wait(tk["kip"])
        i = bank()
        for k in range(4):
            done = mm(R[i][0:NI, 0:C], cip[:, k, :], wvip[:, k, :], k == 0, k == 3, k == 3)
        act.wait(done)
        done = acopy(vipf[0:NI, :], R[i][0:NI, 0:C])
        bank_free[i] = done
        sp.wait(done)
        tk["vipd"] = d_vw.go(vipd, vipf[0:NI, :])
        i = bank()
        pe.wait(tsq)
        for k in range(4):
            done = mm(R[i][:, 0:NI], ones, csq[:, k, :], k == 0, k == 3, k == 3)
        nv = ninv[:].rearrange("p b n -> p (b n)")
        dve.wait(done)
        t = dve.do(lambda e, o=R[i]: e.tensor_scalar(nv, o[:, 0:NI], EPS2, None, ALU.max))
        bank_free[i] = t
        act.wait(t)
        t = act.do(lambda e: e.activation(nv, nv, ACT.Sqrt))
        dve.wait(t)
        t = dve.do(lambda e: e.reciprocal(nv, nv))
        dve.wait(t)
        tk["ninv"] = dve.do(lambda e: e.tensor_scalar(nv, nv, 0.5, None, ALU.mult))
        dve.wait(tk["ninv"])
        pool.wait(tk["ninv"])
        act.wait(tk["ninv"])

        def load_ctx(b):
            i = b % 2
            sp.wait(tk.get(("ctx_free", b - 2)))
            tk["ctx", b] = d_ctx[i].go(cT[i][:, :, 0:T], a["ctxT"][b].rearrange("(k e) t -> e k t", e=128))

        def load_x(b):
            i = b % 2
            sp.wait(tk.get(("q0", b - 2)), tk.get(("xb", b - 2)), tk.get(("x1", b - 2)))
            for k, (c0, n) in enumerate(CT):
                tk["x", b] = d_x[i].go(xT[i][0:n, k, :], a["xT"][c0:c0 + n, S * b:S * b + 128])
            tk["x", b] = d_x[i].go(xn[i][:], a["x"][b])

        kcount, rcount = [0], [0]

        def k_piece(b, l, m):
            c0, _ = MT[m]
            c = cT[b % 2]
            i = bank()
            if l == 0:
                for (w, lo, hi_) in ((wk[0], 0, 128), (wk[1], TEXT0, T)):
                    for k in range(4):
                        done = mm(R[i][:, lo:hi_], w[:, k, c0:c0 + 128], c[:, k, lo:hi_], k == 0, k == 3, k == 3)
                n = T
            else:
                for k in range(4):
                    done = mm(R[i][:, 0:TEXT1], wk[2][:, k, c0:c0 + 128], c[:, k, 0:TEXT1], k == 0, k == 3, k == 3)
                n = TEXT1
            j = kcount[0]
            s = kst[j % 2]
            kcount[0] += 1
            act.wait(done, tk.get(("kst_free", j - 2)))
            hi = acopy(s[:, 0, 0:n], R[i][:, 0:n])
            v = rcount[0]
            rcount[0] += 1
            rem_ = rem[v % 2]
            dve.wait(hi, tk.get(("rem_free", v - 2)))
            r = tt(dve, rem_[:, 0:n], R[i][:, 0:n], s[:, 0, 0:n], ALU.subtract)
            bank_free[i] = r
            tk["last_k_read", b] = done
            if j % 2:
                dve.wait(r)
                mid = vcopy(s[:, 1, 0:n], rem_[:, 0:n])
                pool.wait(mid)
            else:
                act.wait(r)
                mid = acopy(s[:, 1, 0:n], rem_[:, 0:n])
                pool.wait(mid)
            low = tt(pool, s[:, 2, 0:n], rem_[:, 0:n], s[:, 1, 0:n], ALU.subtract)
            tk["rem_free", v] = low
            if l == 1:
                low = pool.do(lambda e, s=s: e.tensor_copy(s[:, :, TEXT1:T], kip[:, m, :, NIP * b:NIP * b + NIP]))
            sp.wait(low)
            r0 = 64 if m == 2 else 0
            tk["kst_free", j] = tk["kw", b, l] = d_kw[l][j % 2].go(
                kd[l][b][:, c0 + r0:c0 + 128, :].rearrange("a r t -> r a t"), s[r0:128, :, :])
            tk["kws", b, l, j % 2] = tk["kw", b, l]

        def k_stack(b, l, parts=(0, 1)):
            for part in parts:
                h0, h1 = HALVES[part]
                sp.wait(tk.get(("kws", b, l, 0)), tk.get(("kws", b, l, 1)))
                sp.wait(tk.get(("st_done", b - 1, l, part)))
                for g in range(6):
                    tk["Ks", b, l, part] = d_kr[l][part].go(
                        Ks[l][D * g:D * g + D, h0:h1, 0:T],
                        kd[l][b, KPART[g], D * h0:D * h1, :].rearrange("(h d) t -> d h t", d=D))

        def split_v(i, n, o, v, free):
            ps = R[i][0:n, 0:C].rearrange("p (h d) -> p h d", d=D)
            rv = rem[v % 2][0:n, 0:C].rearrange("p (h d) -> p h d", d=D)
            act.wait(free)
            hi = acopy(o[:, :, 0:D], ps)
            dve.wait(hi, tk.get(("rem_free", v - 2)))
            r = tt(dve, rv, ps, o[:, :, 0:D], ALU.subtract)
            bank_free[i] = r
            act.wait(r)
            mid = acopy(o[:, :, D:2 * D], rv)
            pool.wait(mid)
            tk["rem_free", v] = tt(pool, o[:, :, 2 * D:3 * D], rv, o[:, :, D:2 * D], ALU.subtract)
            return tk["rem_free", v]

        def v_piece(b, l, t_, text=False):
            c = cT[b % 2]
            n = TEXT0 if text else (119 if l == 0 else 115) if t_ == 2 else 128
            w = wv[2] if l else wv[0] if text else wv[1]
            i = bank()
            for k in range(4):
                done = mm(R[i][0:n, 0:C], c[:, k, 128 * t_:128 * t_ + n], w[:, k, :], k == 0, k == 3, k == 3)
            act.wait(done)
            v = rcount[0]
            rcount[0] += 1
            if l == 1:
                tk["V1", b] = split_v(i, n, V1[b % 2][0:n, t_], v, tk.get(("pv_done", b - 2, 1)))
            elif text:
                tk["V0", b] = split_v(i, n, V0t[:], v, tk.get(("pv_done", b - 1, 0)))
            elif t_:
                tk["V0", b] = split_v(i, n, V0[0:n, t_], v, tk.get(("pv_done", b - 1, 0)))
            else:
                o = V0[:, 0]
                ps = R[i][:, 0:C].rearrange("p (h d) -> p h d", d=D)
                rv = rem[v % 2][:, 0:C].rearrange("p (h d) -> p h d", d=D)
                act.wait(tk.get(("pv_done", b - 1, 0)))
                hi = acopy(o[:, :, 0:D], ps, mip[:, 0:1])
                dve.wait(hi, tk.get(("rem_free", v - 2)))
                r = stt(rv, ps, mip[:, 0:1], o[:, :, 0:D], ALU.mult, ALU.subtract)
                bank_free[i] = r
                act.wait(r)
                mid = acopy(o[:, :, D:2 * D], rv)
                pool.wait(mid)
                tk["rem_free", v] = tt(pool, o[:, :, 2 * D:3 * D], rv, o[:, :, D:2 * D], ALU.subtract)
                tk["V0", b] = tk["rem_free", v]
            tk["ctx_free", b] = done

        def g_piece(b, t_):
            c = cT[b % 2]
            n, w = ROWS[t_], T - 128 * t_
            i = bank()
            first = min(128 * t_, T - 128)
            for k in range(4):
                done = mm(R[i][0:n, first:T], c[:, k, 128 * t_:128 * t_ + n], c[:, k, first:T], k == 0, k == 3, k == 3)
            ps = R[i][0:n, 128 * t_:T]
            tk["ctx_free", b] = done
            gh, gl, o = Gh[b % 2], Gl[b % 2], GO[t_]
            we = w - NIP
            act.wait(done, tk.get(("y_done", b - 2)))
            hi = act.do(lambda e: e.activation(gh[0:n, o:o + n], ps[:, 0:n], ACT.Copy, scale=0.5))
            if we > n:
                hi = acopy(gh[0:n, o + n:o + we], ps[:, n:we])
            hi = acopy(g4[0:n, t_, :], ps[:, we:w])
            dve.wait(hi)
            lo = stt(gl[0:n, o:o + n], ps[:, 0:n], 0.5, gh[0:n, o:o + n].bitcast(fp32), ALU.mult, ALU.subtract)
            if we > n:
                lo = tt(dve, gl[0:n, o + n:o + we], ps[:, n:we], gh[0:n, o + n:o + we].bitcast(fp32), ALU.subtract)
            bank_free[i] = lo
            tk["G", b] = lo
            if t_ == 2:
                act.wait(hi)
                hi = acopy(g4s[:, :, 0, :], g4[:])
                pool.wait(hi)
                r = tt(pool, g4r[:], g4[:], g4s[:, :, 0, :], ALU.subtract)
                pool.wait(r)
                mid = pool.do(lambda e: e.tensor_copy(g4s[:, :, 1, :], g4r[:]))
                pool.wait(mid)
                low = tt(pool, g4s[:, :, 2, :], g4r[:], g4s[:, :, 1, :], ALU.subtract)
                act.wait(low)
                for u in range(3):
                    tk["W4", b] = acopy(V1[b % 2][:, u, :, 49:61],
                                        g4s[:, u, :, :].rearrange("p a n -> p (a n)").unsqueeze(1).to_broadcast([128, H, 12]))
                act.wait(tk["W4", b])

        def q_split(b, l, rhs, token, key):
            i = bank()
            pe.wait(token)
            for m, (c0, _) in enumerate(MT):
                for k, (_, n) in enumerate(CT):
                    done = mm(R[i][:, 128 * m:128 * m + 128], wq[l][0:n, k, c0:c0 + 128], rhs[0:n, k, :], k == 0, k == 2,
                              k == 2 and m == 2)
            tk[key, b] = done
            ps = R[i][:, 0:384].rearrange("p (m q) -> p m q", m=3)[:, :, 0:S]
            act.wait(done, tk.get("qw"))
            hi = acopy(qst[:, :, 0, :], ps, 0.25)
            dve.wait(hi, tk.get("qrem_free"))
            r = stt(qrem[:], ps, 0.25, qst[:, :, 0, :], ALU.mult, ALU.subtract)
            bank_free[i] = r
            dve.wait(r)
            mid = vcopy(qst[:, :, 1, :], qrem[:])
            dve.wait(mid)
            low = tt(dve, qst[:, :, 2, :], qrem[:], qst[:, :, 1, :], ALU.subtract)
            tk["qrem_free"] = low
            sp.wait(low)
            for m, (c0, r0) in enumerate(MT):
                tk["qw"] = d_qw[l].go(qd[l][b][:, c0 + r0:c0 + 128, :].rearrange("a r q -> r a q"), qst[r0:128, m, :, :])
            tk["qw", b, l] = tk["qw"]

        def q_stack(b, l):
            sp.wait(tk["qw", b, l], tk.get(("st_done", b - 1, l, 1)))
            for g in range(6):
                tk["Qs", b, l] = d_qr[l].go(Qs[l][D * g:D * g + D, :, :],
                                            qd[l][b, QPART[g]].rearrange("(h d) q -> d h q", d=D))

        def s_max(b, l, h0, wide):
            n, o = (3, ST) if wide else (2, PN)
            pe.wait(tk["Ks", b, l, 0 if h0 + n <= HALVES[0][1] else 1], tk["Qs", b, l], tk.get(("smax_free", wide)))
            pe.wait(*((tk.get("st_free"),) if wide else (tk.get("pv_free"), tk.get("ns_free"))))
            for u in range(n):
                done = mm(o[0:S, u, 0:T], Qs[l][0:96, h0 + u, :], Ks[l][0:96, h0 + u, 0:T], True, True, u == n - 1)
            dve.wait(done, tk.get("mn"))
            if l == 0:
                dve.do(lambda e: e.reduce_max(m0[:, h0:h0 + n], o[0:S, 0:n, 0:TEXT0], X))
                t_ = dve.do(lambda e: e.reduce_max(m0[:, H + h0:H + h0 + n], o[0:S, 0:n, TEXT0:T], X))
            else:
                dve.wait(tk.get(("fused", b - 2)))
                dve.do(lambda e: e.reduce_max(m1[:, h0:h0 + n], o[0:S, 0:n, 0:TEXT1], X))
                t_ = vcopy(sip[b % 2][:, h0:h0 + n, :], o[0:S, 0:n, TEXT1:T])
            tk["smax_free", wide] = t_
            tk["m", b, l] = t_

        def m_rows(b, l, between):
            n = 2 * H if l == 0 else H
            m_ = m0 if l == 0 else m1
            dve.wait(tk["m", b, l], tk.get("mT"))
            tk["mn"] = dve.do(lambda e: e.tensor_scalar(mn[:, 0:n], m_[:], -1.0, LOG_P, ALU.mult, ALU.add))
            between()
            i = bank()
            pe.wait(tk["mn"])
            done = tk["mT"] = transpose(R[i][0:n, 0:S], mn[:, 0:n], ident[0:S, 0:S], True)
            act.wait(done, tk.get("mrow"))
            hi = acopy(ms[0:n, 0, :], R[i][0:n, 0:S])
            dve.wait(hi)
            r = tt(dve, mrem[0:n, :], R[i][0:n, 0:S], ms[0:n, 0, :], ALU.subtract)
            bank_free[i] = r
            dve.wait(r)
            mid = vcopy(ms[0:n, 1, :], mrem[0:n, :])
            dve.wait(mid)
            low = tt(dve, ms[0:n, 2, :], mrem[0:n, :], ms[0:n, 1, :], ALU.subtract)
            dve.wait(low)
            sp.wait(low, tk.get(("st_done", b - 1, l, 1)))
            for c in range(n // H):
                for u in range(3):
                    r0 = 96 + 3 * c + u
                    tk["mrow"] = d_m[l].go(Qs[l][r0:r0 + 1, :, :], ms[H * c:H * c + H, u, :])
            tk["mrow", b, l] = tk["mrow"]

        gcount = [0]

        def scores(b, l, g):
            rows = 102 if l == 0 else 100
            pe.wait(tk["mrow", b, l], tk.get("st_free"), tk.get(("smax_free", True)))
            for u in range(3):
                for h in range(GH):
                    done = mm(ST[:, u, S * h:S * h + S], Ks[l][0:rows, GH * g + h, 128 * u:128 * u + 128],
                              Qs[l][0:rows, GH * g + h, :], True, True, u == 2 and h == GH - 1)
            if GH * g + GH in (HALVES[0][1], HALVES[1][1]):
                tk["st_done", b, l, 0 if GH * g + GH == HALVES[0][1] else 1] = done
            n = gcount[0]
            gcount[0] += 1
            i = n % 2
            st = ST[:, :, 0:QW]
            p32v, phv = (x[:, 0:3 * QW].rearrange("p (u q) -> p u q", u=3) for x in (p32[i], ph[i]))
            act.wait(done, tk.get(("pl_done", n - 2)), tk.get(("pl_first", n - 2)), tk.get(("w2_done", n - 2)))
            t32 = act.do(lambda e: e.activation(p32v, st, ACT.Exp))
            act.wait(tk.get(("pv", n - 2)))
            th = act.do(lambda e: e.activation(phv, st, ACT.Exp))
            tk["ph", n] = th
            tk["st_free"] = th
            pool.wait(tk["ph", n], tk.get(("pv", n - 2)))
            c = QW if l == 0 else 0
            tk["pl_done", n] = tt(pool, pl[i][:, c:3 * QW], p32[i][:, c:3 * QW], ph[i][:, c:3 * QW], ALU.subtract)
            if c:
                dve.wait(tk["ph", n], tk.get(("pv", n - 2)))
                tk["pl_first", n] = tt(dve, pl[i][:, 0:c], p32[i][:, 0:c], ph[i][:, 0:c], ALU.subtract)
            return n

        def scores_r(n):
            i = n % 2
            act.wait(tk.get("y"), tk.get(("w2_done", n - 1)))
            tk["pr", n] = tk["st_free"] = act.do(lambda e: e.activation(
                pr[:].rearrange("p (u q) -> p u q", u=3), ST[:, :, 0:QW], ACT.Exp))
            dve.wait(tk["pr", n], tk.get(("ns_done", n - 2)))
            tk["w2_done", n] = stt(w2[i][:], p32[i][:], 2.0, pr[:].bitcast(fp32), ALU.mult, ALU.subtract)

        def reduce_parts(o, x):
            return dve.do(lambda e: e.tensor_reduce(o, x, X, ALU.add))

        def pv0(b, g, n):
            i = n % 2
            pe.wait(tk["V0", b], tk["ph", n], tk["pl_done", n], tk["pl_first", n], tk.get("pv_free"), tk.get(("smax_free", False)))
            first = True
            for h in range(GH):
                hh = GH * g + h
                for c in range(2):
                    for u in ((0,) if c == 0 else (0, 1, 2)):
                        k = TEXT0 if c == 0 else 119 if u == 2 else 128
                        v = V0t[0:k, hh, :] if c == 0 else V0[0:k, u, hh, :]
                        for p_ in (ph[i], pl[i]):
                            o = QW * u + S * h
                            last = h == GH - 1 and c == 1 and u == 2 and p_ is pl[i]
                            done = mm(PV[:, 98 * h + 49 * c:98 * h + 49 * c + 49], p_[0:k, o:o + 128], v, first, last,
                                      last, True)
                            first = False
            tk["pv", n] = done
            if g == NG - 1:
                tk["pv_done", b, 0] = done
            ps = PV[0:S, 0:98 * GH].rearrange("p (c f) -> p c f", f=49)
            dve.wait(done, tk.get("acc"))
            z = dve.do(lambda e: e.reciprocal(rz[:].unsqueeze(2), ps[:, :, 48:49]))
            r = reduce_parts(acc[0][:], ps[:, :, 0:48].rearrange("p c (f d) -> p c d f", d=D))
            tk["pv_free"] = r
            dve.wait(r)
            r = tt(dve, acc[1][:], acc[0][:], rz[:].unsqueeze(2).to_broadcast([S, 2 * GH, D]), ALU.mult)
            dve.wait(r, tk.get("o0_free"))
            a2 = acc[1][:].rearrange("p (h c) d -> p c h d", c=2)
            tk["o0"] = tk["acc"] = tt(dve, o0[:, 64 * g:64 * g + 64].rearrange("p (h d) -> p h d", d=D),
                                      a2[:, 0], a2[:, 1], ALU.add)

        def y_part(b, g, n):
            i = n % 2
            pe.wait(tk["G", b], tk["pr", n])
            for j in range(3):
                r_ = bank()
                nj = ROWS[j]
                mms = [(gg, u) for u in range(j + 1) for gg in (Gh[b % 2], Gl[b % 2])]
                for x, (gg, u) in enumerate(mms):
                    o = GO[u] + 128 * (j - u)
                    done = mm(R[r_][0:nj, 0:QW], gg[0:ROWS[u], o:o + nj], pr[0:ROWS[u], QW * u:QW * u + QW],
                              x == 0, x == len(mms) - 1, x == len(mms) - 1)
                dve.wait(done, tk["w2_done", n])
                w = w2[i][0:nj, QW * j:QW * j + QW]
                t_ = tt(dve, w, R[r_][0:nj, 0:QW], w, ALU.mult)
                bank_free[r_] = t_
                tk["prod", j] = t_
            tk["y"] = done
            if g == NG - 1:
                tk["y_done", b] = done

        def ns_part(b, g, n):
            pe.wait(tk.get("ns_free"), tk.get(("smax_free", False)))
            for j in range(3):
                pe.wait(tk["prod", j])
                tk["ns", j] = mm(NS[32 * j:32 * j + 32, 0:QW], sel[0:ROWS[j], g, :], w2[n % 2][0:ROWS[j], QW * j:QW * j + QW],
                                 g == 0, g == NG - 1, True, True)
            tk["ns_done", n] = tk["ns", 2]

        def pv1(b, g, n):
            i = n % 2
            pe.wait(tk["V1", b], tk["W4", b], tk["ph", n], tk["pl_done", n], tk.get("pv_free"),
                    tk.get(("smax_free", False)))
            first = True
            for h in range(GH):
                hh = GH * g + h
                for u in range(3):
                    for p_ in (ph[i], pl[i]):
                        o = QW * u + S * h
                        last = h == GH - 1 and u == 2 and p_ is pl[i]
                        done = mm(PV[:, 61 * h:61 * h + 61], p_[0:ROWS[u], o:o + 128], V1[b % 2][0:ROWS[u], u, hh, :],
                                  first, last, last, True)
                        first = False
            tk["pv", n] = done
            if g == NG - 1:
                tk["pv_done", b, 1] = done
            ps = PV[0:S, 0:61 * GH].rearrange("p (c f) -> p c f", f=61)
            h0 = GH * g
            dve.wait(done, tk.get("num_free"), tk.get("t1_free"), tk.get("acc"))
            vcopy(zs[:, h0:h0 + GH].unsqueeze(2), ps[:, :, 48:49])
            dve.do(lambda e: e.reciprocal(rz[:, 0:GH].unsqueeze(2), ps[:, :, 48:49]))
            reduce_parts(acc[0][:, 0:GH, :], ps[:, :, 0:48].rearrange("p c (f d) -> p c d f", d=D))
            r = reduce_parts(num[:, h0:h0 + GH, :], ps[:, :, 49:61].rearrange("p c (f d) -> p c d f", d=NIP))
            tk["pv_free"] = r
            dve.wait(r)
            tk["t1"] = tk["acc"] = tt(dve, t1[:, 64 * g:64 * g + 64].rearrange("p (h d) -> p h d", d=D), acc[0][:, 0:GH, :],
                                      rz[:, 0:GH].unsqueeze(2).to_broadcast([S, GH, D]), ALU.mult)

        def out_T(src, i_o, token):
            i = bank()
            pe.wait(token)
            for k, (c0, n) in enumerate(CT):
                done = transpose(R[i][0:n, S * k:S * k + S], src[:, c0:c0 + n], ident[0:S, 0:S], k == 2)
            act.wait(done, tk.get(("oT_free", i_o)))
            acopy(oT[i_o][:, 0:2, :], R[i][:, 0:2 * S].rearrange("p (k q) -> p k q", k=2))
            t_ = acopy(oT[i_o][0:64, 2, :], R[i][0:64, 2 * S:3 * S])
            bank_free[i] = t_
            return done, t_

        def out_mm(l, token):
            i = bank()
            pe.wait(token)
            for k, (_, n) in enumerate(CT):
                done = mm(R[i][0:S, 0:C], oT[l][0:n, k, :], wo[l][0:n, k, :], k == 0, k == 2, k == 2)
            tk["oT_free", l] = done
            return i, done

        def finish0(b):
            pool.wait(tk["x", b])
            tk["xb", b] = tt(pool, xn[b % 2][:], xn[b % 2][:], bias[0][:], ALU.add)
            read, t_ = out_T(o0, 0, tk["o0"])
            tk["o0_free"] = read
            yield
            i, done = out_mm(0, t_)
            dve.wait(done, tk["xb", b], tk.get(("out", b - 2)))
            t_ = tt(dve, x1[b % 2][:], R[i][0:S, 0:C], xn[b % 2][:], ALU.add)
            bank_free[i] = t_
            tk["x1", b] = t_
            yield
            i = bank()
            pe.wait(t_)
            for k, (c0, n) in enumerate(CT):
                done = transpose(R[i][0:n, S * k:S * k + S], x1[b % 2][:, c0:c0 + n], ident[0:S, 0:S], k == 2)
            act.wait(done, tk.get(("q1", b - 1)))
            acopy(x1T[:, 0:2, 0:S], R[i][:, 0:2 * S].rearrange("p (k q) -> p k q", k=2))
            t_ = acopy(x1T[0:64, 2, 0:S], R[i][0:64, 2 * S:3 * S])
            bank_free[i] = t_
            pool.wait(done)
            tk["x1b", b] = tt(pool, x1[b % 2][:], x1[b % 2][:], bias[1][:], ALU.add)
            yield
            q_split(b, 1, x1T, t_, "q1")

        def finish1(b):
            sp.wait(tk["vipd"], tk.get(("ip_mm", b - 1)))
            tk["vrep", b] = d_v.go(vbd[:], vipd[NIP * b:NIP * b + NIP, :].rearrange("(a n) c -> a n c", a=1)
                                      .to_broadcast([H, NIP, C]))
            pool.wait(tk["vrep", b])
            tk["vbd", b] = tt(pool, vbd[:], vbd[:], bmask[:], ALU.mult)
            act.wait(tk["ns", 0], tk["ns", 1], tk["ns", 2], tk.get("n2"))
            t_ = acopy(nss[:], NS[0:96, 0:QW])
            tk["ns_free"] = t_
            yield
            i = bank()
            pe.wait(t_)
            for h in range(GH):
                done = mm(R[i][0:S, 128 * h:128 * h + 128], nss[:, S * h:S * h + S],
                          sel2[:].unsqueeze(1).to_broadcast([96, 16, 8]), True, True, h == GH - 1)
            tk["n2"] = done
            dve.wait(tk["t1"])
            z = tt(dve, zq[:], zs[:], zs[:], ALU.mult)
            dve.wait(done, z)
            t_ = stt(d2[:].rearrange("p (g h) -> p g h", h=GH), zq[:].rearrange("p (g h) -> p g h", h=GH), EPS2 / 2,
                     R[i][0:S, :].rearrange("p (h g) -> p g h", g=128)[:, 0:NG, :], ALU.mult, ALU.max)
            bank_free[i] = t_
            act.wait(t_)
            t_ = act.do(lambda e: e.activation(d2[:], d2[:], ACT.Sqrt, scale=2.0))
            dve.wait(t_)
            t_ = dve.do(lambda e: e.reciprocal(sm[0][:], d2[:]))
            dve.wait(t_)
            f0, f1 = fus
            t_ = tt(dve, f0[:], num[:], sm[0][:].unsqueeze(2).to_broadcast([S, H, NIP]), ALU.mult)
            tk["num_free"] = t_
            dve.wait(t_)
            t_ = tt(dve, f1[:], f0[:], ninv[0:S, b, :].unsqueeze(1).to_broadcast([S, H, NIP]), ALU.mult)
            dve.wait(t_)
            t_ = tt(dve, f0[:], f1[:], sip[b % 2][:], ALU.add)
            tk["fused", b] = t_
            dve.wait(t_)
            t_ = dve.do(lambda e: e.reduce_max(sm[1][:], f0[:], X))
            dve.wait(t_)
            t_ = tt(dve, f1[:], f0[:], sm[1][:].unsqueeze(2).to_broadcast([S, H, NIP]), ALU.subtract)
            act.wait(t_)
            t_ = act.do(lambda e: e.activation(f0[:], f1[:], ACT.Exp))
            dve.wait(t_)
            t_ = dve.do(lambda e: e.reduce_sum(sm[1][:], f0[:], X))
            dve.wait(t_)
            t_ = dve.do(lambda e: e.reciprocal(sm[2][:], sm[1][:]))
            dve.wait(t_)
            t_ = dve.do(lambda e: e.tensor_scalar(sm[0][:], sm[2][:], side[:, 0:1], None, ALU.mult))
            dve.wait(t_, tk.get("pr_read"))
            t_ = tt(dve, f1[:], f0[:], sm[0][:].unsqueeze(2).to_broadcast([S, H, NIP]), ALU.mult)
            yield
            i = bank()
            pe.wait(t_)
            done = transpose(R[i][0:H * NIP, 0:S], f1[:].rearrange("p h n -> p (h n)"), ident[0:S, 0:S], True)
            tk["pr_read"] = done
            act.wait(done, tk.get(("ip_mm", b - 1)))
            t_ = acopy(prT[:], R[i][0:H * NIP, 0:S])
            bank_free[i] = t_
            yield
            i = bank()
            pe.wait(t_, tk["vbd", b])
            done = mm(R[i][0:S, 0:C], prT[:], vbd[:], True, True, True)
            tk["ip_mm", b] = done
            dve.wait(done, tk.get("o1_free"))
            t_ = tt(dve, o1[:], R[i][0:S, 0:C], t1[:], ALU.add)
            bank_free[i] = t_
            tk["t1_free"] = t_
            yield
            read, t_ = out_T(o1, 1, t_)
            tk["o1_free"] = read
            yield
            i, done = out_mm(1, t_)
            dve.wait(done, tk["x1b", b])
            t_ = tt(dve, x1[b % 2][:], R[i][0:S, 0:C], x1[b % 2][:], ALU.add)
            bank_free[i] = t_
            sp.wait(t_)
            tk["out", b] = d_out[b % 2].go(out[b], x1[b % 2][:])

        def keys_ahead(b):
            pe.wait(tk["ctx", b])
            for l in range(2):
                for m in range(3):
                    yield k_piece(b, l, m)
            yield q_split(b, 0, xT[b % 2], tk["x", b], "q0")

        def values_ahead(b):
            for t_ in range(3):
                yield v_piece(b, 1, t_)
                yield g_piece(b, t_)
            yield v_piece(b, 0, 0, True)
            for t_ in range(3):
                yield v_piece(b, 0, t_)

        def take(pieces, n):
            for _ in range(n):
                next(pieces, None)

        def groups(b, l, between):
            prev = None
            for g in range(NG + 1):
                n = scores(b, l, g) if g < NG else None
                if l == 0:
                    between(g)
                if g and l == 0:
                    pv0(b, g - 1, prev)
                if g and l == 1:
                    y_part(b, g - 1, prev)
                if l == 1:
                    between(g, False)
                if n is not None and l == 1:
                    scores_r(n)
                if g and l == 1:
                    pv1(b, g - 1, prev)
                    ns_part(b, g - 1, prev)
                if l == 1:
                    between(g, True)
                prev = n

        def maxima(b, l, between):
            for h in range(0, H, 5):
                s_max(b, l, h, True)
                between()
                s_max(b, l, h + 3, False)
                between()
            m_rows(b, l, between)

        load_ctx(0)
        load_ctx(1)
        load_x(0)
        for _ in keys_ahead(0):
            pass
        k_stack(0, 0)
        q_stack(0, 0)
        values = values_ahead(0)
        maxima(0, 0, lambda: take(values, 1))
        take(values, 99)
        for b in range(B + 1):
            if b + 2 < B:
                load_ctx(b + 2)
            keys, values, last = iter(()), iter(()), iter(())
            if b + 1 < B:
                load_x(b + 1)
                keys, values = keys_ahead(b + 1), values_ahead(b + 1)
            first = iter(())
            if b < B:
                groups(b, 0, lambda g: take(keys, 1))
                first = finish0(b)
            if not b:
                take(keys, 99)

            def among(g, end):
                if end and g < 2:
                    take(keys, 1)
                if end or g:
                    take(first, 1)
                if end and g == 2 and b < B:
                    k_stack(b, 1, (0,))
            if b:
                groups(b - 1, 1, among)
                last = finish1(b - 1)
                take(last, 1)
            else:
                k_stack(b, 1, (0,))
            take(first, 99)
            if b + 1 < B:
                k_stack(b + 1, 0)
                q_stack(b + 1, 0)
            if b < B:
                k_stack(b, 1, (1,))
                q_stack(b, 1)
            count = [0]

            def between():
                count[0] += 1
                if count[0] in (1, 6, 8, 10, 12):
                    take(last, 1)
                if count[0] in (2, 3, 5, 7, 9, 11, 14, 16, 18):
                    take(values, 1)
            if b + 1 < B:
                take(values, 1)
            if b + 1 < B:
                maxima(b + 1, 0, between)
            if b < B:
                maxima(b, 1, between)
            take(last, 99)
            take(values, 99)
        sp.wait(tk["out", B - 2], tk["out", B - 1])

        block = ctx.enter_context(nc.Block())

        @block.tensor
        def _(e):
            pe.run(e)

        @block.vector
        def _(e):
            dve.run(e)

        @block.scalar
        def _(e):
            act.run(e)

        @block.gpsimd
        def _(e):
            pool.run(e)

        @block.sync
        def _(e):
            sp.run(e)


def kernel(**inputs):
    import ml_dtypes
    import numpy as np
    import concourse.bacc as bacc
    from concourse.bass_utils import run_bass_kernel_spmd

    x = np.asarray(inputs["x"])
    c = np.asarray(inputs["ctx_2048"])
    g = {k: np.asarray(v) for k, v in inputs.items()}
    xT = np.zeros((C, B * S + 16), np.float32)
    xT[:, 0:B * S] = x.reshape(B * S, C).T
    kones0 = np.zeros((6, KW), ml_dtypes.bfloat16)
    kones0[0:3, 0:TEXT0] = 1
    kones0[3:6, TEXT0:KW] = 1
    kones1 = np.ones((4, KW), ml_dtypes.bfloat16)
    kones1[3, 0:TEXT1] = 0
    kones1[3, TEXT1:KW] = -1e30
    sel = np.zeros((128, NG, 32), np.float32)
    sel2 = np.zeros((96, 8), np.float32)
    for i in range(NG):
        sel[:, i, i] = 1
        sel2[[i, 32 + i, 64 + i], i] = 1
    mip = np.ones((128, 1), np.float32)
    mip[0:TEXT0] = 0
    bmask = np.zeros((H, NIP, H, D), ml_dtypes.bfloat16)
    for h in range(H):
        bmask[h, :, h, :] = 1
    arrays = {
        "x": x,
        "xT": xT,
        "ctxT": c.transpose(0, 2, 1),
        "cip": c[:, TEXT1:].transpose(2, 0, 1).reshape(E, B * NIP),
        "wk0": g["L0_xattn_Wk"].T, "wkip0": g["L0_xattn_Wk_ip"].T, "wk1": g["L1_xattn_W_k"],
        "wv0": g["L0_xattn_Wv"].T, "wvip0": g["L0_xattn_Wv_ip"].T, "wv1": g["L1_xattn_W_v"],
        "wq0": g["L0_xattn_Wq"].T, "wo0": g["L0_xattn_Wo"].T,
        "wq1": g["L1_xattn_W_q"], "wo1": g["L1_xattn_W_out"],
        "wkip1": g["L1_xattn_W_k_ip"], "wvip1": g["L1_xattn_W_v_ip"],
        "bo0": g["L0_xattn_bo"], "bo1": g["L1_xattn_b_out"],
        "side": g["fside_S_0"].reshape(S, 1),
        "ident": np.eye(128, dtype=np.float32),
        "kones0": kones0,
        "kones1": kones1,
        "qone": np.ones((H, S), ml_dtypes.bfloat16),
        "sel": sel, "sel2": sel2, "mip": mip,
        "bmask": bmask.reshape(H * NIP, C),
    }
    arrays = {f"in_{k}": np.ascontiguousarray(v) for k, v in arrays.items()}
    nc = bacc.Bacc("TRN2", target_bir_lowering=False, num_devices=1)
    a = {k[3:]: nc.dram_tensor(k, v.shape, mybir.dt.from_np(v.dtype), kind="ExternalInput").ap() for k, v in arrays.items()}
    out = nc.dram_tensor("out_0", (B, S, C), mybir.dt.float32, kind="ExternalOutput").ap()
    xattn_two_layers(nc, a, out)
    return run_bass_kernel_spmd(nc, [arrays], core_ids=[0]).results[0]["out_0"]
```

```python
from contextlib import ExitStack

import concourse.bass as bass
from concourse import mybir
from concourse.alu_op_type import AluOpType as ALU

B, S, C, T, E = 32, 112, 320, 375, 512
H, D = 20, 16
TEXT0, TEXT1, NIP = 77, 371, 4
KW = 384
GH, NG = 4, 5
QW = GH * S
PADQ = 128 - S
ROWS = [128, 128, 115]
EPS2 = 1e-24
LOG_P = 8.317766166719343
QPART = [0, 1, 2, 0, 1, 0]
KPART = [0, 0, 0, 1, 1, 2]
CT = [(0, 128), (128, 128), (256, 64)]
HALVES = [(0, 12), (12, 20)]
MT = [(0, 0), (128, 0), (192, 64)]


class Queue:

    def __init__(self, sem):
        self.sem, self.n, self.steps, self.reached = sem, 0, [], {}

    def wait(self, *tokens):
        for t in tokens:
            if t is None:
                continue
            sem, value = t
            if self.reached.get(id(sem), 0) < value:
                self.reached[id(sem)] = value
                self.steps.append(lambda e, s=sem, v=value: e.wait_ge(s, v))

    def do(self, f, signal=True):
        if not signal:
            self.steps.append(f)
            return None
        self.n += 1
        self.steps.append(lambda e: f(e).then_inc(self.sem, 1))
        return self.sem, self.n

    def run(self, engine):
        for s in self.steps:
            s(engine)


class Stream:

    def __init__(self, queue, sem):
        self.queue, self.sem, self.n = queue, sem, 0

    def go(self, dst, src):
        self.n += 16
        self.queue.steps.append(lambda e: e.dma_start(dst, src).then_inc(self.sem, 16))
        return self.sem, self.n


def xattn_two_layers(nc, a, out):
    fp32, f32r, bf16, fp16 = mybir.dt.float32, mybir.dt.float32r, mybir.dt.bfloat16, mybir.dt.float16
    ACT, X = mybir.ActivationFunctionType, mybir.AxisListType.X
    ctx = ExitStack()
    with ctx:
        def sb(name, shape, dt=fp32):
            return ctx.enter_context(nc.sbuf_tensor(name, shape, dt))

        def pb(name, shape, dt=fp32):
            return ctx.enter_context(nc.psum_tensor(name, shape, dt))

        def sem(name):
            return ctx.enter_context(nc.semaphore(name))

        kd = [nc.dram_tensor(f"k_split{l}", [B, 3, C, T], bf16, kind="Internal").ap() for l in range(2)]
        qd = [nc.dram_tensor(f"q_split{l}", [B, 3, C, S], bf16, kind="Internal").ap() for l in range(2)]
        vipd = nc.dram_tensor("v_ip", [B * NIP, C], fp32, kind="Internal").ap()

        cT = [sb(f"cT{i}", [128, 4, T + 1]) for i in range(2)]
        wk = [sb(f"wk{i}", [128, 4, n]) for i, n in enumerate((384, 384, 256))]
        wv = [sb(f"wv{i}", [128, 4, C]) for i in range(3)]
        wq = [sb(f"wq{i}", [128, 3, C]) for i in range(2)]
        wo = [sb(f"wo{i}", [128, 3, C]) for i in range(2)]
        Ks = [sb(f"Ks{i}", [102, H, KW], bf16) for i in range(2)]
        Qs = [sb(f"Qs{i}", [102, H, S], bf16) for i in range(2)]
        kst = [sb(f"kst{i}", [128, 3, T], bf16) for i in range(2)]
        rem = [sb(f"rem{i}", [128, T]) for i in range(2)]
        qst = sb("qst", [128, 3, 3, S], bf16)
        qrem = sb("qrem", [128, 3, S])
        V0t = sb("V0t", [TEXT0, H, 49], bf16)
        V0 = sb("V0", [128, 3, H, 49], bf16)
        V1 = [sb(f"V1{i}", [128, 3, H, 61], bf16) for i in range(2)]
        g4 = sb("g4", [128, 3, NIP])
        g4r = sb("g4r", [128, 3, NIP])
        g4s = sb("g4s", [128, 3, 3, NIP], bf16)
        GO = [0, T - NIP, T - NIP + 243]
        Gh = [sb(f"Gh{i}", [128, 729], f32r) for i in range(2)]
        Gl = [sb(f"Gl{i}", [128, 729], f32r) for i in range(2)]
        p32 = [sb(f"p32_{i}", [128, 3 * QW]) for i in range(2)]
        ph = [sb(f"ph_{i}", [128, 3 * QW + PADQ], fp16) for i in range(2)]
        pl = [sb(f"pl_{i}", [128, 3 * QW + PADQ], fp16) for i in range(2)]
        pr = sb("pr", [128, 3 * QW], f32r)
        w2 = [sb(f"w2_{i}", [128, 3 * QW]) for i in range(2)]
        xn = [sb(f"xn{i}", [S, C]) for i in range(2)]
        xT = [sb(f"xT{i}", [128, 3, 128]) for i in range(2)]
        x1 = [sb(f"x1_{i}", [S, C]) for i in range(2)]
        x1T = sb("x1T", [128, 3, 128])
        oT = [sb(f"oT{i}", [128, 3, S]) for i in range(2)]
        o0 = sb("o0", [S, C])
        o1 = sb("o1", [S, C])
        t1 = sb("t1", [S, C])
        acc = [sb(f"acc{i}", [S, 2 * GH, D]) for i in range(2)]
        rz = sb("rz", [S, 2 * GH])
        m0 = sb("m0", [S, 2 * H])
        m1 = sb("m1", [S, H])
        mn = sb("mn", [S, 2 * H])
        mrem = sb("mrem", [2 * H, S])
        ms = sb("ms", [2 * H, 3, S], bf16)
        sip = [sb(f"sip{i}", [S, H, NIP]) for i in range(2)]
        num = sb("num", [S, H, NIP])
        zs = sb("zs", [S, H])
        zq = sb("zq", [S, H])
        nss = sb("nss", [96, QW])
        d2 = sb("d2", [S, H])
        fus = [sb(f"fus{i}", [S, H, NIP]) for i in range(2)]
        sm = [sb(f"sm{i}", [S, H]) for i in range(3)]
        prT = sb("prT", [H * NIP, S])
        vbd = sb("vbd", [H * NIP, C])
        NI = B * NIP
        kip = sb("kip", [128, 3, 3, NI], bf16)
        ninv = sb("ninv", [128, B, NIP])
        side = sb("side", [S, 1])
        ident = sb("ident_sb", [128, 128])
        sel = sb("sel_sb", [128, NG, 32])
        sel2 = sb("sel2_sb", [96, 8])
        mip = sb("mip_sb", [128, 1])
        bmask = sb("bmask_sb", [H * NIP, C], bf16)
        wkip = p32[0][:, 0:4 * C].rearrange("p (k c) -> p k c", k=4)
        wvip = p32[1][:, 0:4 * C].rearrange("p (k c) -> p k c", k=4)
        cip = w2[0][:, 0:4 * NI].rearrange("p (k c) -> p k c", k=4)
        csq = w2[1][:, 0:4 * NI].rearrange("p (k c) -> p k c", k=4)
        vipf = w2[1][:, 512:512 + C]
        ones = w2[1][:, 896:1024]

        ST = pb("ST", [128, 3, 512])
        PN = pb("PN", [128, 2, 512])
        PV, NS = PN[:, 0, :], PN[:, 1, :]
        R = [pb(f"R{i}", [128, 512]) for i in range(3)]

        pe, dve, act, pool, sp = (Queue(sem(n)) for n in ("s_pe", "s_dve", "s_act", "s_pool", "s_sp"))
        d_ctx = [Stream(sp, sem(f"d_ctx{i}")) for i in range(2)]
        d_x = [Stream(sp, sem(f"d_x{i}")) for i in range(2)]
        d_kw = [[Stream(sp, sem(f"d_kw{l}{i}")) for i in range(2)] for l in range(2)]
        d_kr = [[Stream(sp, sem(f"d_kr{l}{i}")) for i in range(2)] for l in range(2)]
        d_qw = [Stream(sp, sem(f"d_qw{i}")) for i in range(2)]
        d_qr = [Stream(sp, sem(f"d_qr{i}")) for i in range(2)]
        d_m = [Stream(sp, sem(f"d_m{i}")) for i in range(2)]
        d_vw = Stream(sp, sem("d_vw"))
        d_v = Stream(sp, sem("d_v"))
        d_out = [Stream(sp, sem(f"d_out{i}")) for i in range(2)]

        tk = {}
        bank_free = [None, None, None]
        bank_at = [0]

        def bank():
            i = bank_at[0] % 3
            bank_at[0] += 1
            pe.wait(bank_free[i])
            return i

        def mm(o, l, r, start, stop, signal=False, shared=False):
            return pe.do(lambda e: e.matmul(o, l, r, start=start, stop=stop, skip_group_check=shared), signal)

        def transpose(o, i, idn, signal=False):
            return pe.do(lambda e: e.transpose(o, i, idn), signal)

        def vcopy(o, i):
            return dve.do(lambda e: e.tensor_copy(o, i))

        def acopy(o, i, scale=1.0):
            return act.do(lambda e: e.activation(o, i, ACT.Copy, scale=scale))

        def tt(q, o, x, y, op):
            return q.do(lambda e: e.tensor_tensor(o, x, y, op))

        def stt(o, x, s, y, op0, op1):
            return dve.do(lambda e: e.scalar_tensor_tensor(out=o, in0=x, scalar=s, in1=y, op0=op0, op1=op1))

        def load(key, *pairs):
            st = Stream(sp, sem(f"d_{key}"))
            for dst, src in pairs:
                tk[key] = st.go(dst, src)

        def rows(name):
            return a[name].rearrange("(k e) c -> e k c", e=128)

        def clear_pads():
            for t_ in Ks:
                tk["pads"] = pool.do(lambda e, t_=t_: e.memset(t_[:, :, 360:KW], 0.0))
            pool.do(lambda e: e.memset(V0t[:, :, 48:49], 1.0))
            tk["v_ones"] = pool.do(lambda e: e.memset(V0[:, 1:3, :, 48:49], 1.0))
            for i in range(2):
                pool.do(lambda e, t_=V1[i]: e.memset(t_[:, :, :, 48:49], 1.0))
                for t_ in (ph[i], pl[i]):
                    pool.do(lambda e, t_=t_: e.memset(t_[:, :], 0.0))
                tk["oT_ones"] = dve.do(lambda e, t_=oT[i]: e.memset(t_[64:65, 2, :], 1.0))
            pool.do(lambda e: e.memset(g4[:], 0.0))
            tk["pool_sets"] = pool.do(lambda e: e.memset(x1T[:], 0.0))

        def image_tokens():
            dve.wait(tk["cip"])
            tsq = tt(dve, csq, cip, cip, ALU.mult)
            t = dve.do(lambda e: e.memset(ones, 1.0))
            pe.wait(tk["cip"], tk["wkip1"])
            for m, (c0, _) in enumerate(MT):
                i = bank()
                for k in range(4):
                    done = mm(R[i][:, 0:NI], wkip[:, k, c0:c0 + 128], cip[:, k, :], k == 0, k == 3, k == 3)
                act.wait(done)
                hi = acopy(kip[:, m, 0, :], R[i][:, 0:NI])
                dve.wait(hi, tk.get(("rem_free", rcount[0] - 2)), tk.get(("rem_free", rcount[0] - 1)))
                r = tt(dve, rem[0][:, 0:NI], R[i][:, 0:NI], kip[:, m, 0, :], ALU.subtract)
                bank_free[i] = r
                dve.wait(r)
                mid = vcopy(kip[:, m, 1, :], rem[0][:, 0:NI])
                dve.wait(mid)
                tk["kip"] = tt(dve, kip[:, m, 2, :], rem[0][:, 0:NI], kip[:, m, 1, :], ALU.subtract)
                dve.wait(tk["kip"])
            pool.wait(tk["kip"])
            i = bank()
            pe.wait(tk["wvip1"])
            for k in range(4):
                done = mm(R[i][0:NI, 0:C], cip[:, k, :], wvip[:, k, :], k == 0, k == 3, k == 3)
            act.wait(done)
            done = acopy(vipf[0:NI, :], R[i][0:NI, 0:C])
            bank_free[i] = done
            sp.wait(done)
            tk["vipd"] = d_vw.go(vipd, vipf[0:NI, :])
            i = bank()
            pe.wait(tsq, t)
            for k in range(4):
                done = mm(R[i][:, 0:NI], ones, csq[:, k, :], k == 0, k == 3, k == 3)
            nv = ninv[:].rearrange("p b n -> p (b n)")
            dve.wait(done)
            t = dve.do(lambda e, o=R[i]: e.tensor_scalar(nv, o[:, 0:NI], EPS2, None, ALU.max))
            bank_free[i] = t
            act.wait(t)
            t = act.do(lambda e: e.activation(nv, nv, ACT.Sqrt))
            dve.wait(t)
            t = dve.do(lambda e: e.reciprocal(nv, nv))
            dve.wait(t)
            t = dve.do(lambda e: e.tensor_scalar(nv, nv, 0.5, None, ALU.mult))
            dve.wait(t)
            act.wait(t, tk["vipd"])

        def load_ctx(b):
            i = b % 2
            sp.wait(tk.get(("ctx_free", b - 2)))
            tk["ctx", b] = d_ctx[i].go(cT[i][:, :, 0:T], a["ctxT"][b].rearrange("(k e) t -> e k t", e=128))

        def load_x(b):
            i = b % 2
            sp.wait(tk.get(("q0", b - 2)), tk.get(("x1", b - 2)))
            d_x[i].go(xT[i][:], a["xT"][:, S * b:S * b + 128].rearrange("(k e) s -> e k s", e=128))
            tk["x", b] = d_x[i].go(xn[i][:], a["x"][b])

        kcount, rcount = [0], [0]

        def k_piece(b, l, m):
            c0 = 256 if l is None else 128 * m
            c = cT[b % 2]
            i = bank()
            if l == 1:
                pe.wait(tk["wk1"])
                for k in range(4):
                    done = mm(R[i][:, 0:TEXT1], wk[2][:, k, c0:c0 + 128], c[:, k, 0:TEXT1], k == 0, k == 3, k == 3)
                n = TEXT1
            else:
                for (w, lo, hi_, key) in ((wk[0], 0, 128, "wk0"), (wk[1], TEXT0, T, "wkip0")):
                    pe.wait(tk[key])
                    for k in range(4):
                        done = mm(R[i][:, lo:hi_], w[:, k, c0:c0 + 128], c[:, k, lo:hi_], k == 0, k == 3,
                                  k == 3 and hi_ == T, True)
                n = T
            j = kcount[0]
            s = kst[j % 2]
            kcount[0] += 1
            act.wait(done, *tk.get(("kst_free", j - 2), ()))
            hi = acopy(s[:, 0, 0:n], R[i][:, 0:n])
            v = rcount[0]
            rcount[0] += 1
            rem_ = rem[v % 2]
            dve.wait(hi, tk.get(("rem_free", v - 2)))
            r = tt(dve, rem_[:, 0:n], R[i][:, 0:n], s[:, 0, 0:n], ALU.subtract)
            bank_free[i] = r
            tk["last_k_read", b] = done
            if j % 2:
                dve.wait(r)
                mid = vcopy(s[:, 1, 0:n], rem_[:, 0:n])
                pool.wait(mid)
            else:
                act.wait(r)
                mid = acopy(s[:, 1, 0:n], rem_[:, 0:n])
                pool.wait(mid)
            low = tt(pool, s[:, 2, 0:n], rem_[:, 0:n], s[:, 1, 0:n], ALU.subtract)
            tk["rem_free", v] = low
            if l != 0:
                r0, mk = (64, 2) if l is None else (0, m)
                pool.wait(low, tk["kip"])
                low = pool.do(lambda e, s=s: e.tensor_copy(s[r0:128, :, TEXT1:T],
                                                           kip[r0:128, mk, :, NIP * b:NIP * b + NIP]))
                pool.wait(low)
            sp.wait(low)
            tk["kst_free", j] = []
            for l_, r0, r1 in (((0, 0, 64), (1, 64, 128)) if l is None else ((l, 0, 128),)):
                tk["kws", b, l_, j % 2] = d_kw[l_][j % 2].go(
                    kd[l_][b][:, c0:c0 + r1 - r0, :].rearrange("a r t -> r a t"), s[r0:r1, :, :])
                tk["kst_free", j].append(tk["kws", b, l_, j % 2])

        def k_stack(b, l, parts=(0, 1)):
            for part in parts:
                h0, h1 = HALVES[part]
                sp.wait(tk.get(("kws", b, l, 0)), tk.get(("kws", b, l, 1)))
                sp.wait(tk.get(("st_done", b - 1, l, part)))
                for g in range(6):
                    tk["Ks", b, l, part] = d_kr[l][part].go(
                        Ks[l][D * g:D * g + D, h0:h1, 0:T],
                        kd[l][b, KPART[g], D * h0:D * h1, :].rearrange("(h d) t -> d h t", d=D))

        later = []

        def flush():
            now = later[:]
            later.clear()
            for f in now:
                f()

        def split_v(i, n, o, key, free, scale=1.0, early=False):
            v = rcount[0]
            rcount[0] += 1
            ps = R[i][0:n, 0:C].rearrange("p (h d) -> p h d", d=D)
            rv = rem[v % 2][0:n, 0:C].rearrange("p (h d) -> p h d", d=D)
            act.wait(free, tk.get(("rem_free", v - 2)))
            acopy(rv, ps, scale)
            whole = acopy(o[:, :, 0:D], ps, scale)
            bank_free[i] = whole
            q = dve if early else pool
            q.wait(whole)
            r = tt(q, rv, rv, o[:, :, 0:D], ALU.subtract)

            def rest():
                act.wait(r)
                mid = acopy(o[:, :, D:2 * D], rv)
                pool.wait(mid)
                tk["rem_free", v] = tk[key] = tt(pool, o[:, :, 2 * D:3 * D], rv, o[:, :, D:2 * D], ALU.subtract)
            later.append(rest)

        def v_piece(b, l, t_, text=False):
            c = cT[b % 2]
            n = TEXT0 if text else (119 if l == 0 else 115) if t_ == 2 else 128
            w, key = (wv[2], "wv1") if l else (wv[0], "wv0") if text else (wv[1], "wvip0")
            i = bank()
            pe.wait(tk[key])
            for k in range(4):
                done = mm(R[i][0:n, 0:C], c[:, k, 128 * t_:128 * t_ + n], w[:, k, :], k == 0, k == 3, k == 3)
            flush()
            act.wait(done)
            if l == 1:
                split_v(i, n, V1[b % 2][0:n, t_], ("V1", b), tk.get(("pv_done", b - 2, 1)))
            else:
                o, scale = (V0t, 1.0) if text else (V0[0:n, t_], 1.0 if t_ else mip[:, 0:1])
                split_v(i, n, o, ("V0", b), tk.get(("pv_done", b - 1, 0)), scale, text or t_ == 0)
            tk["ctx_free", b] = done

        def g_piece(b, t_):
            c = cT[b % 2]
            n, w = ROWS[t_], T - 128 * t_
            i = bank()
            first = min(128 * t_, T - 128)
            for k in range(4):
                done = mm(R[i][0:n, first:T], c[:, k, 128 * t_:128 * t_ + n], c[:, k, first:T], k == 0, k == 3, k == 3)
            ps = R[i][0:n, 128 * t_:T]
            tk["ctx_free", b] = done
            gh, gl, o = Gh[b % 2], Gl[b % 2], GO[t_]
            we = w - NIP
            act.wait(done, tk.get(("y_done", b - 2)))
            hi = act.do(lambda e: e.activation(gh[0:n, o:o + n], ps[:, 0:n], ACT.Copy, scale=0.5))
            if we > n:
                hi = acopy(gh[0:n, o + n:o + we], ps[:, n:we])
            hi = acopy(g4[0:n, t_, :], ps[:, we:w])
            dve.wait(hi)
            lo = stt(gl[0:n, o:o + n], ps[:, 0:n], 0.5, gh[0:n, o:o + n].bitcast(fp32), ALU.mult, ALU.subtract)
            if we > n:
                lo = tt(dve, gl[0:n, o + n:o + we], ps[:, n:we], gh[0:n, o + n:o + we].bitcast(fp32), ALU.subtract)
            bank_free[i] = lo
            tk["G", b] = lo
            if t_ == 2:
                def rest():
                    act.wait(hi, tk.get("g4s"))
                    h = acopy(g4s[:, :, 0, :], g4[:])
                    pool.wait(h)
                    r = tt(pool, g4r[:], g4[:], g4s[:, :, 0, :], ALU.subtract)
                    pool.wait(r)
                    mid = pool.do(lambda e: e.tensor_copy(g4s[:, :, 1, :], g4r[:]))
                    pool.wait(mid)
                    low = tt(pool, g4s[:, :, 2, :], g4r[:], g4s[:, :, 1, :], ALU.subtract)

                    def last():
                        act.wait(low)
                        for u in range(3):
                            tk["W4", b] = tk["g4s"] = acopy(
                                V1[b % 2][:, u, :, 49:61],
                                g4s[:, u, :, :].rearrange("p a n -> p (a n)").unsqueeze(1).to_broadcast([128, H, 12]))
                    later.append(last)
                later.append(rest)

        def q_split(b, l, rhs, token, key):
            i = bank()
            pe.wait(token, tk["wq0"] if l == 0 else tk["wq1"])
            for m, (c0, _) in enumerate(MT):
                for k, (_, n) in enumerate(CT):
                    done = mm(R[i][:, 128 * m:128 * m + 128], wq[l][0:n, k, c0:c0 + 128], rhs[0:n, k, :], k == 0, k == 2,
                              k == 2 and m == 2)
            tk[key, b] = done
            ps = R[i][:, 0:384].rearrange("p (m q) -> p m q", m=3)[:, :, 0:S]
            act.wait(done, tk.get("qw"))
            hi = acopy(qst[:, :, 0, :], ps, 0.25)
            dve.wait(hi, tk.get("qrem_free"))
            r = stt(qrem[:], ps, 0.25, qst[:, :, 0, :], ALU.mult, ALU.subtract)
            bank_free[i] = r
            dve.wait(r)
            mid = vcopy(qst[:, :, 1, :], qrem[:])
            dve.wait(mid)
            low = tt(dve, qst[:, :, 2, :], qrem[:], qst[:, :, 1, :], ALU.subtract)
            tk["qrem_free"] = low
            sp.wait(low)
            for m, (c0, r0) in enumerate(MT):
                tk["qw"] = d_qw[l].go(qd[l][b][:, c0 + r0:c0 + 128, :].rearrange("a r q -> r a q"), qst[r0:128, m, :, :])
            tk["qw", b, l] = tk["qw"]

        def q_stack(b, l):
            sp.wait(tk["qw", b, l], tk.get(("st_done", b - 1, l, 1)))
            for g in range(6):
                tk["Qs", b, l] = d_qr[l].go(Qs[l][D * g:D * g + D, :, :],
                                            qd[l][b, QPART[g]].rearrange("(h d) q -> d h q", d=D))

        def s_max(b, l, h0, wide):
            n, o = (3, ST) if wide else (2, PN)
            pe.wait(tk["Ks", b, l, 0 if h0 + n <= HALVES[0][1] else 1], tk["Qs", b, l], tk.get(("smax_free", wide)))
            pe.wait(*((tk.get("st_free"),) if wide else (tk.get("pv_free"), tk.get("ns_free"))))
            for u in range(n):
                done = mm(o[0:S, u, 0:T], Qs[l][0:96, h0 + u, :], Ks[l][0:96, h0 + u, 0:T], True, True, u == n - 1)
            dve.wait(done, tk.get("mn"))
            if l == 0:
                dve.do(lambda e: e.reduce_max(m0[:, h0:h0 + n], o[0:S, 0:n, 0:TEXT0], X))
                t_ = dve.do(lambda e: e.reduce_max(m0[:, H + h0:H + h0 + n], o[0:S, 0:n, TEXT0:T], X))
            else:
                dve.wait(tk.get(("fused", b - 2)))
                dve.do(lambda e: e.reduce_max(m1[:, h0:h0 + n], o[0:S, 0:n, 0:TEXT1], X))
                t_ = vcopy(sip[b % 2][:, h0:h0 + n, :], o[0:S, 0:n, TEXT1:T])
            tk["smax_free", wide] = t_
            tk["m", b, l] = t_

        def m_rows(b, l):
            n = 2 * H if l == 0 else H
            m_ = m0 if l == 0 else m1
            dve.wait(tk["m", b, l], tk.get("mT"))
            tk["mn"] = dve.do(lambda e: e.tensor_scalar(mn[:, 0:n], m_[:], -1.0, LOG_P, ALU.mult, ALU.add))
            yield
            i = bank()
            pe.wait(tk["mn"])
            done = tk["mT"] = transpose(R[i][0:n, 0:S], mn[:, 0:n], ident[0:S, 0:S], True)
            act.wait(done, tk.get("mrow"))
            acopy(mrem[0:n, :], R[i][0:n, 0:S])
            hi = acopy(ms[0:n, 0, :], R[i][0:n, 0:S])
            bank_free[i] = hi
            yield
            dve.wait(hi)
            r = tt(dve, mrem[0:n, :], mrem[0:n, :], ms[0:n, 0, :], ALU.subtract)
            dve.wait(r)
            mid = vcopy(ms[0:n, 1, :], mrem[0:n, :])
            dve.wait(mid)
            low = tt(dve, ms[0:n, 2, :], mrem[0:n, :], ms[0:n, 1, :], ALU.subtract)
            dve.wait(low)
            sp.wait(low, tk.get(("st_done", b - 1, l, 1)))
            for c in range(n // H):
                for u in range(3):
                    r0 = 96 + 3 * c + u
                    tk["mrow"] = d_m[l].go(Qs[l][r0:r0 + 1, :, :], ms[H * c:H * c + H, u, :])
            tk["mrow", b, l] = tk["mrow"]

        gcount = [0]

        def scores(b, l, g):
            rows = 102 if l == 0 else 100
            pe.wait(tk["mrow", b, l], tk.get("st_free"), tk.get(("smax_free", True)))
            for u in range(3):
                for h in range(GH):
                    done = mm(ST[:, u, S * h:S * h + S], Ks[l][0:rows, GH * g + h, 128 * u:128 * u + 128],
                              Qs[l][0:rows, GH * g + h, :], True, True, u == 2 and h == GH - 1)
            if GH * g + GH in (HALVES[0][1], HALVES[1][1]):
                tk["st_done", b, l, 0 if GH * g + GH == HALVES[0][1] else 1] = done
            n = gcount[0]
            gcount[0] += 1
            i = n % 2
            st = ST[:, :, 0:QW]
            p32v, phv = (x[:, 0:3 * QW].rearrange("p (u q) -> p u q", u=3) for x in (p32[i], ph[i]))
            act.wait(done, tk.get(("pl_done", n - 2)), tk.get(("pl_first", n - 2)), tk.get(("w2_done", n - 2)))
            t32 = act.do(lambda e: e.activation(p32v, st, ACT.Exp))
            act.wait(tk.get(("pv", n - 2)))
            th = act.do(lambda e: e.activation(phv, st, ACT.Exp))
            tk["ph", n] = th
            tk["st_free"] = th
            pool.wait(tk["ph", n], tk.get(("pv", n - 2)))
            c = QW if l == 0 else 0
            tk["pl_done", n] = tt(pool, pl[i][:, c:3 * QW], p32[i][:, c:3 * QW], ph[i][:, c:3 * QW], ALU.subtract)
            if c:
                dve.wait(tk["ph", n], tk.get(("pv", n - 2)))
                tk["pl_first", n] = tt(dve, pl[i][:, 0:c], p32[i][:, 0:c], ph[i][:, 0:c], ALU.subtract)
            return n

        def scores_r(n):
            i = n % 2
            act.wait(tk.get("y"), tk.get(("w2_done", n - 1)))
            tk["pr", n] = tk["st_free"] = act.do(lambda e: e.activation(
                pr[:].rearrange("p (u q) -> p u q", u=3), ST[:, :, 0:QW], ACT.Exp))
            dve.wait(tk["pr", n], tk.get(("ns_done", n - 2)))
            tk["w2_done", n] = stt(w2[i][:], p32[i][:], 2.0, pr[:].bitcast(fp32), ALU.mult, ALU.subtract)

        def reduce_parts(o, x):
            return dve.do(lambda e: e.tensor_reduce(o, x, X, ALU.add))

        def pv0(b, g, n):
            i = n % 2
            pe.wait(tk["V0", b], tk["ph", n], tk["pl_done", n], tk["pl_first", n], tk.get("pv_free"), tk.get(("smax_free", False)))
            first = True
            for h in range(GH):
                hh = GH * g + h
                for c in range(2):
                    for u in ((0,) if c == 0 else (0, 1, 2)):
                        k = TEXT0 if c == 0 else 119 if u == 2 else 128
                        v = V0t[0:k, hh, :] if c == 0 else V0[0:k, u, hh, :]
                        for p_ in (ph[i], pl[i]):
                            o = QW * u + S * h
                            last = h == GH - 1 and c == 1 and u == 2 and p_ is pl[i]
                            done = mm(PV[:, 98 * h + 49 * c:98 * h + 49 * c + 49], p_[0:k, o:o + 128], v, first, last,
                                      last, True)
                            first = False
            tk["pv", n] = done
            if g == NG - 1:
                tk["pv_done", b, 0] = done
            ps = PV[0:S, 0:98 * GH].rearrange("p (c f) -> p c f", f=49)
            dve.wait(done, tk.get("acc"))
            z = dve.do(lambda e: e.reciprocal(rz[:].unsqueeze(2), ps[:, :, 48:49]))
            r = reduce_parts(acc[0][:], ps[:, :, 0:48].rearrange("p c (f d) -> p c d f", d=D))
            tk["pv_free"] = r
            dve.wait(r)
            r = tt(dve, acc[1][:], acc[0][:], rz[:].unsqueeze(2).to_broadcast([S, 2 * GH, D]), ALU.mult)
            dve.wait(r, tk.get("o0_free"))
            a2 = acc[1][:].rearrange("p (h c) d -> p c h d", c=2)
            tk["o0"] = tk["acc"] = tt(dve, o0[:, 64 * g:64 * g + 64].rearrange("p (h d) -> p h d", d=D),
                                      a2[:, 0], a2[:, 1], ALU.add)

        def y_part(b, g, n):
            i = n % 2
            pe.wait(tk["G", b], tk["pr", n])
            for j in range(3):
                r_ = bank()
                nj = ROWS[j]
                mms = [(gg, u) for u in range(j + 1) for gg in (Gh[b % 2], Gl[b % 2])]
                for x, (gg, u) in enumerate(mms):
                    o = GO[u] + 128 * (j - u)
                    done = mm(R[r_][0:nj, 0:QW], gg[0:ROWS[u], o:o + nj], pr[0:ROWS[u], QW * u:QW * u + QW],
                              x == 0, x == len(mms) - 1, x == len(mms) - 1)
                dve.wait(done, tk["w2_done", n])
                w = w2[i][0:nj, QW * j:QW * j + QW]
                t_ = tt(dve, w, R[r_][0:nj, 0:QW], w, ALU.mult)
                bank_free[r_] = t_
                tk["prod", j] = t_
            tk["y"] = done
            if g == NG - 1:
                tk["y_done", b] = done

        def ns_part(b, g, n):
            pe.wait(tk.get("ns_free"), tk.get(("smax_free", False)))
            for j in range(3):
                pe.wait(tk["prod", j])
                tk["ns", j] = mm(NS[32 * j:32 * j + 32, 0:QW], sel[0:ROWS[j], g, :], w2[n % 2][0:ROWS[j], QW * j:QW * j + QW],
                                 g == 0, g == NG - 1, True, True)
            tk["ns_done", n] = tk["ns", 2]

        def pv1(b, g, n):
            i = n % 2
            pe.wait(tk["V1", b], tk["W4", b], tk["ph", n], tk["pl_done", n], tk.get("pv_free"),
                    tk.get(("smax_free", False)))
            first = True
            for h in range(GH):
                hh = GH * g + h
                for u in range(3):
                    for p_ in (ph[i], pl[i]):
                        o = QW * u + S * h
                        last = h == GH - 1 and u == 2 and p_ is pl[i]
                        done = mm(PV[:, 61 * h:61 * h + 61], p_[0:ROWS[u], o:o + 128], V1[b % 2][0:ROWS[u], u, hh, :],
                                  first, last, last, True)
                        first = False
            tk["pv", n] = done
            if g == NG - 1:
                tk["pv_done", b, 1] = done
            ps = PV[0:S, 0:61 * GH].rearrange("p (c f) -> p c f", f=61)
            h0 = GH * g
            dve.wait(done, tk.get("num_free"), tk.get("t1_free"), tk.get("acc"))
            vcopy(zs[:, h0:h0 + GH].unsqueeze(2), ps[:, :, 48:49])
            dve.do(lambda e: e.reciprocal(rz[:, 0:GH].unsqueeze(2), ps[:, :, 48:49]))
            reduce_parts(acc[0][:, 0:GH, :], ps[:, :, 0:48].rearrange("p c (f d) -> p c d f", d=D))
            r = reduce_parts(num[:, h0:h0 + GH, :], ps[:, :, 49:61].rearrange("p c (f d) -> p c d f", d=NIP))
            tk["pv_free"] = r
            dve.wait(r)
            tk["t1"] = tk["acc"] = tt(dve, t1[:, 64 * g:64 * g + 64].rearrange("p (h d) -> p h d", d=D), acc[0][:, 0:GH, :],
                                      rz[:, 0:GH].unsqueeze(2).to_broadcast([S, GH, D]), ALU.mult)

        def out_T(src, i_o, token):
            i = bank()
            pe.wait(token)
            for k, (c0, n) in enumerate(CT):
                done = transpose(R[i][0:n, S * k:S * k + S], src[:, c0:c0 + n], ident[0:S, 0:S], k == 2)
            act.wait(done, tk.get(("oT_free", i_o)))
            acopy(oT[i_o][:, 0:2, :], R[i][:, 0:2 * S].rearrange("p (k q) -> p k q", k=2))
            t_ = acopy(oT[i_o][0:64, 2, :], R[i][0:64, 2 * S:3 * S])
            bank_free[i] = t_
            return done, t_

        def out_mm(l, token):
            i = bank()
            pe.wait(token, tk["wo0"] if l == 0 else tk["wo1"])
            for k, n in enumerate((128, 128, 65)):
                done = mm(R[i][0:S, 0:C], oT[l][0:n, k, :], wo[l][0:n, k, :], k == 0, k == 2, k == 2)
            tk["oT_free", l] = done
            return i, done

        def finish0(b):
            read, t_ = out_T(o0, 0, tk["o0"])
            tk["o0_free"] = read
            yield
            i, done = out_mm(0, t_)
            dve.wait(done, tk["x", b], tk.get(("out", b - 2)))
            t_ = tt(dve, x1[b % 2][:], R[i][0:S, 0:C], xn[b % 2][:], ALU.add)
            bank_free[i] = t_
            tk["x1", b] = t_
            yield
            i = bank()
            pe.wait(t_)
            for k, (c0, n) in enumerate(CT):
                done = transpose(R[i][0:n, S * k:S * k + S], x1[b % 2][:, c0:c0 + n], ident[0:S, 0:S], k == 2)
            act.wait(done, tk.get(("q1", b - 1)))
            acopy(x1T[:, 0:2, 0:S], R[i][:, 0:2 * S].rearrange("p (k q) -> p k q", k=2))
            t_ = acopy(x1T[0:64, 2, 0:S], R[i][0:64, 2 * S:3 * S])
            bank_free[i] = t_
            tk["x1T", b] = done
            yield
            q_split(b, 1, x1T, t_, "q1")

        def finish1(b):
            sp.wait(tk["vipd"], tk.get(("ip_mm", b - 1)))
            tk["vrep", b] = d_v.go(vbd[:], vipd[NIP * b:NIP * b + NIP, :].rearrange("(a n) c -> a n c", a=1)
                                      .to_broadcast([H, NIP, C]))
            pool.wait(tk["vrep", b])
            tk["vbd", b] = tt(pool, vbd[:], vbd[:], bmask[:], ALU.mult)
            act.wait(tk["ns", 0], tk["ns", 1], tk["ns", 2], tk.get("n2"))
            t_ = acopy(nss[:], NS[0:96, 0:QW])
            tk["ns_free"] = t_
            yield
            i = bank()
            pe.wait(t_)
            for h in range(GH):
                done = mm(R[i][0:S, 128 * h:128 * h + 128], nss[:, S * h:S * h + S],
                          sel2[:].unsqueeze(1).to_broadcast([96, 16, 8]), True, True, h == GH - 1)
            tk["n2"] = done
            dve.wait(tk["t1"])
            z = tt(dve, zq[:], zs[:], zs[:], ALU.mult)
            dve.wait(done, z)
            t_ = stt(d2[:].rearrange("p (g h) -> p g h", h=GH), zq[:].rearrange("p (g h) -> p g h", h=GH), EPS2 / 2,
                     R[i][0:S, :].rearrange("p (h g) -> p g h", g=128)[:, 0:NG, :], ALU.mult, ALU.max)
            bank_free[i] = t_
            act.wait(t_)
            t_ = act.do(lambda e: e.activation(d2[:], d2[:], ACT.Sqrt, scale=2.0))
            yield
            dve.wait(t_)
            t_ = dve.do(lambda e: e.reciprocal(sm[0][:], d2[:]))
            dve.wait(t_)
            f0, f1 = fus
            t_ = tt(dve, f0[:], num[:], sm[0][:].unsqueeze(2).to_broadcast([S, H, NIP]), ALU.mult)
            tk["num_free"] = t_
            dve.wait(t_)
            t_ = tt(dve, f1[:], f0[:], ninv[0:S, b, :].unsqueeze(1).to_broadcast([S, H, NIP]), ALU.mult)
            dve.wait(t_)
            t_ = tt(dve, f0[:], f1[:], sip[b % 2][:], ALU.add)
            tk["fused", b] = t_
            dve.wait(t_)
            t_ = dve.do(lambda e: e.reduce_max(sm[1][:], f0[:], X))
            dve.wait(t_)
            t_ = tt(dve, f1[:], f0[:], sm[1][:].unsqueeze(2).to_broadcast([S, H, NIP]), ALU.subtract)
            act.wait(t_)
            t_ = act.do(lambda e: e.activation(f0[:], f1[:], ACT.Exp))
            yield
            dve.wait(t_)
            t_ = dve.do(lambda e: e.reduce_sum(sm[1][:], f0[:], X))
            dve.wait(t_)
            t_ = dve.do(lambda e: e.reciprocal(sm[2][:], sm[1][:]))
            dve.wait(t_)
            t_ = dve.do(lambda e: e.tensor_scalar(sm[0][:], sm[2][:], side[:, 0:1], None, ALU.mult))
            dve.wait(t_, tk.get("pr_read"))
            t_ = tt(dve, f1[:], f0[:], sm[0][:].unsqueeze(2).to_broadcast([S, H, NIP]), ALU.mult)
            yield
            i = bank()
            pe.wait(t_)
            done = transpose(R[i][0:H * NIP, 0:S], f1[:].rearrange("p h n -> p (h n)"), ident[0:S, 0:S], True)
            tk["pr_read"] = done
            act.wait(done, tk.get(("ip_mm", b - 1)))
            t_ = acopy(prT[:], R[i][0:H * NIP, 0:S])
            bank_free[i] = t_
            yield
            i = bank()
            pe.wait(t_, tk["vbd", b])
            done = mm(R[i][0:S, 0:C], prT[:], vbd[:], True, True, True)
            tk["ip_mm", b] = done
            dve.wait(done, tk.get("o1_free"))
            t_ = tt(dve, o1[:], R[i][0:S, 0:C], t1[:], ALU.add)
            bank_free[i] = t_
            tk["t1_free"] = t_
            yield
            read, t_ = out_T(o1, 1, t_)
            tk["o1_free"] = read
            yield
            i, done = out_mm(1, t_)
            dve.wait(done, tk["x1T", b])
            t_ = tt(dve, x1[b % 2][:], R[i][0:S, 0:C], x1[b % 2][:], ALU.add)
            bank_free[i] = t_
            sp.wait(t_)
            tk["out", b] = d_out[b % 2].go(out[b], x1[b % 2][:])

        def ahead(b):
            pe.wait(tk["ctx", b])
            for l, m in ((0, 0), (0, 1), (None, 0), (1, 0)):
                yield k_piece(b, l, m)
            yield q_split(b, 0, xT[b % 2], tk["x", b], "q0")
            yield k_piece(b, 1, 1)
            yield from values_ahead(b)

        def values_ahead(b):
            yield v_piece(b, 0, 0, True)
            for t_ in range(3):
                yield v_piece(b, 0, t_)
            for t_ in range(3):
                yield v_piece(b, 1, t_)
                yield g_piece(b, t_)

        def take(pieces, n):
            for _ in range(n):
                next(pieces, None)

        def groups(b, l, between):
            prev = None
            for g in range(NG + 1):
                n = scores(b, l, g) if g < NG else None
                if l == 0:
                    between(g)
                if g and l == 0:
                    pv0(b, g - 1, prev)
                if g and l == 1:
                    y_part(b, g - 1, prev)
                if l == 1:
                    between(g, False)
                if n is not None and l == 1:
                    scores_r(n)
                if g and l == 1:
                    pv1(b, g - 1, prev)
                    ns_part(b, g - 1, prev)
                if l == 1:
                    between(g, True)
                prev = n

        def maxima(b, l, between):
            for h in range(0, H, 5):
                s_max(b, l, h, True)
                between()
                s_max(b, l, h + 3, False)
                between()
            return m_rows(b, l)

        clear_pads()
        load("wk0", (wk[0][:], rows("wk0")))
        load_ctx(0)
        load("wkip0", (wk[1][:], rows("wkip0")))
        load("cip", (cip, rows("cip")))
        load("wkip1", (wkip, rows("wkip1")))
        load_x(0)
        load("wq0", (wq[0][:], rows("wq0")))
        load("mip", (mip[:], a["mip"]))
        load("ident", (ident[:], a["ident"]))
        load("wk1", (wk[2][:], rows("wk1")))
        load("wvip1", (wvip, rows("wvip1")))
        load("wv1", (wv[2][:], rows("wv1")))
        for t_ in (act, pe, dve):
            t_.wait(tk["pool_sets"])
        pe.wait(tk["ctx", 0])
        for m in range(2):
            k_piece(0, 0, m)
        image_tokens()
        k_piece(0, None, 0)
        q_split(0, 0, xT[0], tk["x", 0], "q0")
        sp.wait(tk["pads"])
        load("ones_rows", (Ks[0][96:102, :, :], a["kones0"]), (Ks[1][96:100, :, :], a["kones1"]),
             (Qs[1][99:100, :, :], a["qone"].rearrange("(a h) q -> a h q", a=1)))
        pe.wait(tk["ones_rows"])
        k_stack(0, 0)
        q_stack(0, 0)
        load("wv0", (wv[0][:], rows("wv0")))
        load("wvip0", (wv[1][:], rows("wvip0")))
        load("wo0", (wo[0][:], rows("wo0")))
        load("wq1", (wq[1][:], rows("wq1")))
        load("wo1", (wo[1][:], rows("wo1")))
        load_ctx(1)
        load("small", (sel[:], a["sel"]), (sel2[:], a["sel2"]), (bmask[:], a["bmask"]), (side[:], a["side"]))
        dve.wait(tk["mip"])
        tk["v_mask"] = vcopy(V0[:, 0, :, 48:49], mip[:].unsqueeze(1).to_broadcast([128, H, 1]))
        act.wait(tk["mip"])
        for m in range(2):
            k_piece(0, 1, m)
        pe.wait(tk["ident"], tk["v_mask"], tk["oT_ones"])
        values = values_ahead(0)
        rows0 = maxima(0, 0, lambda: take(values, 1))
        take(values, 99)
        take(rows0, 9)
        flush()
        flush()
        for t_ in (pe, dve, pool):
            t_.wait(tk["small"])
        rows1 = iter(())
        for b in range(B + 1):
            if b + 2 < B:
                load_ctx(b + 2)
            pieces = iter(())
            if b + 1 < B:
                load_x(b + 1)
                pieces = ahead(b + 1)
            first, last = iter(()), iter(())

            def among0(g):
                take(rows1, 1)
                take(pieces, 1)
                if g < 2:
                    flush()

            def among1(g, end):
                if g == 0:
                    take(pieces, 1)
                if end or g:
                    take(first, 1)
                if end and g == 2 and b < B:
                    k_stack(b, 1, (0,))

            if b < B:
                groups(b, 0, among0)
                first = finish0(b)
            take(rows1, 9)
            if not b:
                take(pieces, 2)
            if b + 1 < B:
                k_stack(b + 1, 0)
                q_stack(b + 1, 0)
            if b:
                groups(b - 1, 1, among1)
                last = finish1(b - 1)
                take(last, 1)
            else:
                k_stack(b, 1, (0,))
            take(first, 99)
            if b < B:
                k_stack(b, 1, (1,))
                q_stack(b, 1)
            count = [0]
            rows0 = iter(())

            def between():
                count[0] += 1
                if count[0] > 9:
                    take(rows0, 1)
                if count[0] in (1, 2, 3, 6, 8, 10, 12):
                    take(last, 1)
                if count[0] in (2, 4, 6, 8, 10, 12, 14, 16):
                    take(pieces, 1)
            if b + 1 < B:
                rows0 = maxima(b + 1, 0, between)
                take(rows0, 1)
            if b < B:
                rows1 = maxima(b, 1, between)
                take(rows1, 1)
            take(rows0, 9)
            take(last, 99)
            take(pieces, 99)
        sp.wait(tk["out", B - 2], tk["out", B - 1])

        block = ctx.enter_context(nc.Block())

        @block.tensor
        def _(e):
            pe.run(e)

        @block.vector
        def _(e):
            dve.run(e)

        @block.scalar
        def _(e):
            act.run(e)

        @block.gpsimd
        def _(e):
            pool.run(e)

        @block.sync
        def _(e):
            sp.run(e)


def kernel(**inputs):
    import ml_dtypes
    import numpy as np
    import concourse.bacc as bacc
    from concourse.bass_utils import run_bass_kernel_spmd

    x = np.asarray(inputs["x"])
    c = np.asarray(inputs["ctx_2048"])
    g = {k: np.asarray(v) for k, v in inputs.items()}
    wk1 = g["L1_xattn_W_k"]

    def padded(w, *below):
        o = np.zeros((384, C), np.float32)
        o[0:C] = w
        for r in below:
            o[C] = r
        return o

    xT = np.zeros((384, B * S + 16), np.float32)
    xT[0:C, 0:B * S] = x.reshape(B * S, C).T
    kones0 = np.zeros((6, KW), ml_dtypes.bfloat16)
    kones0[0:3, 0:TEXT0] = 1
    kones0[3:6, TEXT0:KW] = 1
    kones1 = np.ones((4, KW), ml_dtypes.bfloat16)
    kones1[3, 0:TEXT1] = 0
    kones1[3, TEXT1:KW] = -1e30
    sel = np.zeros((128, NG, 32), np.float32)
    sel2 = np.zeros((96, 8), np.float32)
    for i in range(NG):
        sel[:, i, i] = 1
        sel2[[i, 32 + i, 64 + i], i] = 1
    mip = np.ones((128, 1), np.float32)
    mip[0:TEXT0] = 0
    bmask = np.zeros((H, NIP, H, D), ml_dtypes.bfloat16)
    for h in range(H):
        bmask[h, :, h, :] = 1
    arrays = {
        "x": x,
        "xT": xT,
        "ctxT": c.transpose(0, 2, 1),
        "cip": c[:, TEXT1:].transpose(2, 0, 1).reshape(E, B * NIP),
        "wk0": np.concatenate([g["L0_xattn_Wk"].T, wk1[:, 256:]], 1),
        "wkip0": np.concatenate([g["L0_xattn_Wk_ip"].T, wk1[:, 256:]], 1), "wk1": wk1[:, 0:256],
        "wv0": g["L0_xattn_Wv"].T, "wvip0": g["L0_xattn_Wv_ip"].T, "wv1": g["L1_xattn_W_v"],
        "wq0": padded(g["L0_xattn_Wq"].T), "wo0": padded(g["L0_xattn_Wo"].T, g["L0_xattn_bo"]),
        "wq1": padded(g["L1_xattn_W_q"]), "wo1": padded(g["L1_xattn_W_out"], g["L1_xattn_b_out"]),
        "wkip1": g["L1_xattn_W_k_ip"], "wvip1": g["L1_xattn_W_v_ip"],
        "side": g["fside_S_0"].reshape(S, 1),
        "ident": np.eye(128, dtype=np.float32),
        "kones0": np.repeat(kones0[:, None], H, 1),
        "kones1": np.repeat(kones1[:, None], H, 1),
        "qone": np.ones((H, S), ml_dtypes.bfloat16),
        "sel": sel, "sel2": sel2, "mip": mip,
        "bmask": bmask.reshape(H * NIP, C),
    }
    arrays = {f"in_{k}": np.ascontiguousarray(v) for k, v in arrays.items()}
    nc = bacc.Bacc("TRN2", target_bir_lowering=False, num_devices=1)
    a = {k[3:]: nc.dram_tensor(k, v.shape, mybir.dt.from_np(v.dtype), kind="ExternalInput").ap() for k, v in arrays.items()}
    out = nc.dram_tensor("out_0", (B, S, C), mybir.dt.float32, kind="ExternalOutput").ap()
    xattn_two_layers(nc, a, out)
    return run_bass_kernel_spmd(nc, [arrays], core_ids=[0]).results[0]["out_0"]
```

```python
from contextlib import ExitStack

import concourse.bass as bass
from concourse import mybir
from concourse.alu_op_type import AluOpType as ALU

B, S, C, T, E = 32, 112, 320, 375, 512
H, D = 20, 16
TEXT0, TEXT1, NIP = 77, 371, 4
KW = 384
GH, NG = 4, 5
QW = GH * S
PADQ = 128 - S
ROWS = [128, 128, 115]
EPS2 = 1e-24
LOG_P = 8.317766166719343
QPART = [0, 1, 2, 0, 1, 0]
KPART = [0, 0, 0, 1, 1, 2]
CT = [(0, 128), (128, 128), (256, 64)]
HALVES = [(0, 12), (12, 20)]
MT = [(0, 0), (128, 0), (192, 64)]


class Queue:

    def __init__(self, sem):
        self.sem, self.n, self.steps, self.reached = sem, 0, [], {}

    def wait(self, *tokens):
        for t in tokens:
            if t is None:
                continue
            sem, value = t
            if self.reached.get(id(sem), 0) < value:
                self.reached[id(sem)] = value
                self.steps.append(lambda e, s=sem, v=value: e.wait_ge(s, v))

    def do(self, f, signal=True):
        if not signal:
            self.steps.append(f)
            return None
        self.n += 1
        self.steps.append(lambda e: f(e).then_inc(self.sem, 1))
        return self.sem, self.n

    def run(self, engine):
        for s in self.steps:
            s(engine)


class Stream:

    def __init__(self, queue, sem):
        self.queue, self.sem, self.n = queue, sem, 0

    def go(self, dst, src, queue=None):
        self.n += 16
        (queue or self.queue).steps.append(lambda e: e.dma_start(dst, src).then_inc(self.sem, 16))
        return self.sem, self.n


def xattn_two_layers(nc, a, out):
    fp32, f32r, bf16, fp16 = mybir.dt.float32, mybir.dt.float32r, mybir.dt.bfloat16, mybir.dt.float16
    ACT, X = mybir.ActivationFunctionType, mybir.AxisListType.X
    ctx = ExitStack()
    with ctx:
        def sb(name, shape, dt=fp32):
            return ctx.enter_context(nc.sbuf_tensor(name, shape, dt))

        def pb(name, shape, dt=fp32):
            return ctx.enter_context(nc.psum_tensor(name, shape, dt))

        def sem(name):
            return ctx.enter_context(nc.semaphore(name))

        kd = [nc.dram_tensor(f"k_split{l}", [B, 3, C, T], bf16, kind="Internal").ap() for l in range(2)]
        qd = [nc.dram_tensor(f"q_split{l}", [B, 3, C, S], bf16, kind="Internal").ap() for l in range(2)]
        vipd = nc.dram_tensor("v_ip", [B * NIP, C], fp32, kind="Internal").ap()

        cT = [sb(f"cT{i}", [128, 4, T + 1]) for i in range(2)]
        wk = [sb(f"wk{i}", [128, 4, n]) for i, n in enumerate((384, 384, 256))]
        wvh = [sb(f"wvh{i}", [128, 4, C], f32r) for i in range(3)]
        wvl = [sb(f"wvl{i}", [128, 4, C], f32r) for i in range(3)]
        ch = [sb(f"ch{i}", [128, 4, 128], f32r) for i in range(2)]
        cl = [sb(f"cl{i}", [128, 4, 128], f32r) for i in range(2)]
        wq = [sb(f"wq{i}", [128, 3, C]) for i in range(2)]
        wo = [sb(f"wo{i}", [128, 3, C]) for i in range(2)]
        Ks = [sb(f"Ks{i}", [102, H, KW], bf16) for i in range(2)]
        Qs = [sb(f"Qs{i}", [102, H, S], bf16) for i in range(2)]
        kst = [sb(f"kst{i}", [128, 3, T], bf16) for i in range(2)]
        rem = [sb(f"rem{i}", [128, T]) for i in range(2)]
        qst = sb("qst", [128, 3, 3, S], bf16)
        qrem = sb("qrem", [128, 3, S])
        V0t = sb("V0t", [TEXT0, H, 49], bf16)
        V0 = sb("V0", [128, 3, H, 49], bf16)
        V1 = sb("V1", [128, 3, H, 61], bf16)
        g4 = sb("g4", [128, 3, NIP])
        g4r = sb("g4r", [128, 3, NIP])
        g4s = sb("g4s", [128, 3, 3, NIP], bf16)
        GO = [0, T - NIP, T - NIP + 243]
        Gh = sb("Gh", [128, 729], f32r)
        Gl = sb("Gl", [128, 729], f32r)
        p32 = [sb(f"p32_{i}", [128, 3 * QW]) for i in range(2)]
        ph = [sb(f"ph_{i}", [128, 3 * QW + PADQ], fp16) for i in range(2)]
        pl = [sb(f"pl_{i}", [128, 3 * QW + PADQ], fp16) for i in range(2)]
        pr = sb("pr", [128, 3 * QW], f32r)
        w2 = [sb(f"w2_{i}", [128, 3 * QW]) for i in range(2)]
        xn = sb("xn", [S, C])
        xT = sb("xT", [128, 3, 128])
        x1 = [sb(f"x1_{i}", [S, C]) for i in range(2)]
        x1T = sb("x1T", [128, 3, 128])
        oT = x1T[:, :, 0:S]
        o0 = t1 = sb("o", [S, C])
        acc = [sb(f"acc{i}", [S, 2 * GH, D]) for i in range(2)]
        rz = sb("rz", [S, 2 * GH])
        m0 = sb("m0", [S, 2 * H])
        m1 = sb("m1", [S, H])
        mn = sb("mn", [S, 2 * H])
        mrem = sb("mrem", [2 * H, S])
        ms = sb("ms", [2 * H, 3, S], bf16)
        sip = [sb(f"sip{i}", [S, H, NIP]) for i in range(2)]
        num = sb("num", [S, H, NIP])
        zs = sb("zs", [S, H])
        zq = sb("zq", [S, H])
        d2 = sb("d2", [S, H])
        dsum = sb("dsum", [S, H])
        fus = [sb(f"fus{i}", [S, H, NIP]) for i in range(2)]
        sm = [sb(f"sm{i}", [S, H]) for i in range(3)]
        prT = sb("prT", [H * NIP, S])
        vbd = sb("vbd", [H * NIP, C])
        NI = B * NIP
        kip = sb("kip", [128, 3, 3, NI], bf16)
        ninv = sb("ninv", [128, B, NIP])
        side = sb("side", [S, 1])
        ident = sb("ident_sb", [128, 128])
        sel = sb("sel_sb", [128, NG, 32])
        mip = sb("mip_sb", [128, 1])
        bmask = sb("bmask_sb", [H * NIP, C], bf16)
        nss = w2[0][0:96, 0:QW]
        wkip = p32[0][:, 0:4 * C].rearrange("p (k c) -> p k c", k=4)
        wvip = p32[1][:, 0:4 * C].rearrange("p (k c) -> p k c", k=4)
        wv0raw = w2[0][:, 0:4 * C].rearrange("p (k c) -> p k c", k=4)
        cip = w2[1][:, 512:512 + 4 * NI].rearrange("p (k c) -> p k c", k=4)
        csq = w2[1][:, 0:4 * NI].rearrange("p (k c) -> p k c", k=4)
        ones = w2[1][:, 1024:1152]
        vipf = cT[1][:, 0, 0:C]

        ST = pb("ST", [128, 3, 512])
        PN = pb("PN", [128, 2, 512])
        PV, NS = PN[:, 0, :], PN[:, 1, :]
        R = [pb(f"R{i}", [128, 512]) for i in range(3)]

        pe, dve, act, pool, sp = (Queue(sem(n)) for n in ("s_pe", "s_dve", "s_act", "s_pool", "s_sp"))
        d_ctx = [Stream(sp, sem(f"d_ctx{i}")) for i in range(2)]
        d_x = Stream(sp, sem("d_x"))
        d_xn = Stream(sp, sem("d_xn"))
        d_kw = [[Stream(sp, sem(f"d_kw{l}{i}")) for i in range(2)] for l in range(2)]
        d_kr = [[Stream(sp, sem(f"d_kr{l}{i}")) for i in range(2)] for l in range(2)]
        d_qw = [Stream(sp, sem(f"d_qw{i}")) for i in range(2)]
        d_qr = [Stream(sp, sem(f"d_qr{i}")) for i in range(2)]
        d_m = [Stream(sp, sem(f"d_m{i}")) for i in range(2)]
        d_vw = Stream(sp, sem("d_vw"))
        d_v = Stream(sp, sem("d_v"))
        d_out = [Stream(sp, sem(f"d_out{i}")) for i in range(2)]

        tk = {}
        bank_free = [None, None, None]
        bank_at = [0]

        def bank():
            i = bank_at[0] % 3
            bank_at[0] += 1
            pe.wait(bank_free[i])
            return i

        def mm(o, l, r, start, stop, signal=False, shared=False):
            return pe.do(lambda e: e.matmul(o, l, r, start=start, stop=stop, skip_group_check=shared), signal)

        def transpose(o, i, idn, signal=False):
            return pe.do(lambda e: e.transpose(o, i, idn), signal)

        def vcopy(o, i):
            return dve.do(lambda e: e.tensor_copy(o, i))

        def acopy(o, i, scale=1.0):
            return act.do(lambda e: e.activation(o, i, ACT.Copy, scale=scale))

        def tt(q, o, x, y, op):
            return q.do(lambda e: e.tensor_tensor(o, x, y, op))

        def stt(o, x, s, y, op0, op1):
            return dve.do(lambda e: e.scalar_tensor_tensor(out=o, in0=x, scalar=s, in1=y, op0=op0, op1=op1))

        def load(key, *pairs):
            st = Stream(sp, sem(f"d_{key}"))
            for dst, src in pairs:
                tk[key] = st.go(dst, src)

        def rows(name):
            return a[name].rearrange("(k e) c -> e k c", e=128)

        def clear_pads():
            for t_ in Ks:
                tk["pads"] = pool.do(lambda e, t_=t_: e.memset(t_[:, :, 360:KW], 0.0))
            pool.do(lambda e: e.memset(V0t[:, :, 48:49], 1.0))
            tk["v_ones"] = pool.do(lambda e: e.memset(V0[:, 1:3, :, 48:49], 1.0))
            pool.do(lambda e: e.memset(V1[:, :, :, 48:49], 1.0))
            for i in range(2):
                for t_ in (ph[i], pl[i]):
                    pool.do(lambda e, t_=t_: e.memset(t_[:, :], 0.0))
            pool.do(lambda e: e.memset(g4[:], 0.0))
            tk["pool_sets"] = pool.do(lambda e: e.memset(x1T[:], 0.0))
            dve.wait(tk["pool_sets"])
            tk["oT_ones"] = dve.do(lambda e: e.memset(x1T[64:65, 2, :], 1.0))

        def image_keys():
            pe.wait(tk["cip"], tk["wkip1"])
            for m, (c0, _) in enumerate(MT):
                i = bank()
                for k in range(4):
                    done = mm(R[i][:, 0:NI], wkip[:, k, c0:c0 + 128], cip[:, k, :], k == 0, k == 3, k == 3)
                act.wait(done)
                hi = acopy(kip[:, m, 0, :], R[i][:, 0:NI])
                dve.wait(hi, tk.get(("rem_free", rcount[0] - 2)), tk.get(("rem_free", rcount[0] - 1)))
                r = tt(dve, rem[0][:, 0:NI], R[i][:, 0:NI], kip[:, m, 0, :], ALU.subtract)
                bank_free[i] = r
                dve.wait(r)
                mid = vcopy(kip[:, m, 1, :], rem[0][:, 0:NI])
                dve.wait(mid)
                tk["kip"] = tt(dve, kip[:, m, 2, :], rem[0][:, 0:NI], kip[:, m, 1, :], ALU.subtract)
                dve.wait(tk["kip"])
            tk["wkip_read"] = done

        def image_values():
            dve.wait(tk["cip"])
            tsq = tt(dve, csq, cip, cip, ALU.mult)
            t = dve.do(lambda e: e.memset(ones, 1.0))
            i = bank()
            pe.wait(tk["wvip1"])
            for k in range(4):
                done = mm(R[i][0:NI, 0:C], cip[:, k, :], wvip[:, k, :], k == 0, k == 3, k == 3)
            tk["wvip_read"] = done
            act.wait(done)
            done = acopy(vipf[0:NI, :], R[i][0:NI, 0:C])
            bank_free[i] = done
            sp.wait(done)
            tk["vipd"] = d_vw.go(vipd, vipf[0:NI, :])
            i = bank()
            pe.wait(tsq, t)
            for k in range(4):
                done = mm(R[i][:, 0:NI], ones, csq[:, k, :], k == 0, k == 3, k == 3)
            nv = ninv[:].rearrange("p b n -> p (b n)")
            dve.wait(done)
            t = dve.do(lambda e, o=R[i]: e.tensor_scalar(nv, o[:, 0:NI], EPS2, None, ALU.max))
            bank_free[i] = t
            act.wait(t)
            t = act.do(lambda e: e.activation(nv, nv, ACT.Sqrt))
            dve.wait(t)
            t = dve.do(lambda e: e.reciprocal(nv, nv))
            dve.wait(t)
            t = dve.do(lambda e: e.tensor_scalar(nv, nv, 0.5, None, ALU.mult))
            dve.wait(t)
            act.wait(t)

        def load_ctx(b, queue):
            i = b % 2
            queue.wait(tk.get(("ctx_free", b - 2)), *tk.get(("ctx_read", b - 2), ()))
            tk["ctx", b] = d_ctx[i].go(cT[i][:, :, 0:T], a["ctxT"][b].rearrange("(k e) t -> e k t", e=128), queue)

        def load_xT(b):
            sp.wait(tk.get(("q0", b - 1)))
            tk["xT", b] = d_x.go(xT[:], a["xT"][:, S * b:S * b + 128].rearrange("(k e) s -> e k s", e=128))

        def load_xn(b):
            sp.wait(tk.get(("x1", b - 1)))
            tk["xn", b] = d_xn.go(xn[:], a["x"][b])

        kcount, rcount = [0], [0]

        def k_piece(b, l, m):
            c0 = 256 if l is None else 128 * m
            c = cT[b % 2]
            i = bank()
            if l == 1:
                pe.wait(tk["wk1"])
                for k in range(4):
                    done = mm(R[i][:, 0:TEXT1], wk[2][:, k, c0:c0 + 128], c[:, k, 0:TEXT1], k == 0, k == 3, k == 3)
                n = TEXT1
            else:
                for (w, lo, hi_, key) in ((wk[0], 0, 128, "wk0"), (wk[1], TEXT0, T, "wkip0")):
                    pe.wait(tk[key])
                    for k in range(4):
                        done = mm(R[i][:, lo:hi_], w[:, k, c0:c0 + 128], c[:, k, lo:hi_], k == 0, k == 3,
                                  k == 3 and hi_ == T, True)
                n = T
            j = kcount[0]
            s = kst[j % 2]
            kcount[0] += 1
            act.wait(done, *tk.get(("kst_free", j - 2), ()))
            hi = acopy(s[:, 0, 0:n], R[i][:, 0:n])
            v = rcount[0]
            rcount[0] += 1
            rem_ = rem[v % 2]
            dve.wait(hi, tk.get(("rem_free", v - 2)))
            r = tt(dve, rem_[:, 0:n], R[i][:, 0:n], s[:, 0, 0:n], ALU.subtract)
            bank_free[i] = r
            tk["last_k_read", b] = done
            if j % 2:
                dve.wait(r)
                mid = vcopy(s[:, 1, 0:n], rem_[:, 0:n])
                pool.wait(mid)
            else:
                act.wait(r)
                mid = acopy(s[:, 1, 0:n], rem_[:, 0:n])
                pool.wait(mid)
            low = tt(pool, s[:, 2, 0:n], rem_[:, 0:n], s[:, 1, 0:n], ALU.subtract)
            tk["rem_free", v] = low
            if l != 0:
                r0, mk = (64, 2) if l is None else (0, m)
                pool.wait(low, tk["kip"])
                low = pool.do(lambda e, s=s: e.tensor_copy(s[r0:128, :, TEXT1:T],
                                                           kip[r0:128, mk, :, NIP * b:NIP * b + NIP]))
                pool.wait(low)
            sp.wait(low)
            tk["kst_free", j] = []
            for l_, r0, r1 in (((0, 0, 64), (1, 64, 128)) if l is None else ((l, 0, 128),)):
                tk["kws", b, l_, j % 2] = d_kw[l_][j % 2].go(
                    kd[l_][b][:, c0:c0 + r1 - r0, :].rearrange("a r t -> r a t"), s[r0:r1, :, :])
                tk["kst_free", j].append(tk["kws", b, l_, j % 2])

        def k_stack(b, l, parts=(0, 1)):
            for part in parts:
                h0, h1 = HALVES[part]
                sp.wait(tk.get(("kws", b, l, 0)), tk.get(("kws", b, l, 1)))
                sp.wait(tk.get(("st_done", b - 1, l, part)))
                for g in range(6):
                    tk["Ks", b, l, part] = d_kr[l][part].go(
                        Ks[l][D * g:D * g + D, h0:h1, 0:T],
                        kd[l][b, KPART[g], D * h0:D * h1, :].rearrange("(h d) t -> d h t", d=D))

        later = []

        def flush():
            now = later[:]
            later.clear()
            for f in now:
                f()

        def split_v(i, n, o, key, free, scale=1.0, early=False):
            v = rcount[0]
            rcount[0] += 1
            ps = R[i][0:n, 0:C].rearrange("p (h d) -> p h d", d=D)
            rv = rem[v % 2][0:n, 0:C].rearrange("p (h d) -> p h d", d=D)
            act.wait(free, tk.get(("rem_free", v - 2)))
            acopy(rv, ps, scale)
            whole = acopy(o[:, :, 0:D], ps, scale)
            bank_free[i] = whole
            q = dve if early else pool
            q.wait(whole)
            r = tt(q, rv, rv, o[:, :, 0:D], ALU.subtract)

            def rest():
                act.wait(r)
                mid = acopy(o[:, :, D:2 * D], rv)
                pool.wait(mid)
                tk["rem_free", v] = tk[key] = tt(pool, o[:, :, 2 * D:3 * D], rv, o[:, :, D:2 * D], ALU.subtract)
            later.append(rest)

        def v_products(j, w, n):
            h, lo, wh, wl = ch[j % 2], cl[j % 2], wvh[w], wvl[w]
            i = bank()
            pe.wait(tk["wvp", w], tk["parts", j])
            for k in range(4):
                for x, (c_, w_) in enumerate(((h, wh), (lo, wh), (h, wl))):
                    end = k == 3 and x == 2
                    done = mm(R[i][0:n, 0:C], c_[:, k, 0:n], w_[:, k, :], k == 0 and x == 0, end, end)
            return done, i

        def text_values(b):
            done, i = v_products(vcount[0], 2, TEXT0)
            flush()
            act.wait(done)
            split_v(i, TEXT0, V0t, ("V0", b), tk.get(("pv_done", b - 1, 0)), early=True)

        vcount = [0]

        def token_parts(j, b, l, t_, q):
            n = 119 if t_ == 2 else 128
            c = cT[b % 2][:, :, 128 * t_:128 * t_ + n]
            h, lo = ch[j % 2][:, :, 0:n], cl[j % 2][:, :, 0:n]
            first = act if q is pool else q
            first.wait(tk["ctx", b], tk.get(("parts_free", j - 2)))
            t = acopy(h, c) if q is pool else vcopy(h, c)
            q.wait(t)
            tk["parts", j] = tt(q, lo, c, h.bitcast(fp32), ALU.subtract)
            tk["ctx_read", b] = [*tk.get(("ctx_read", b), ()), tk["parts", j]]

        def v_piece(b, l, t_, ahead):
            n = (119 if l == 0 else 115) if t_ == 2 else 128
            j = vcount[0]
            vcount[0] += 1
            done, i = v_products(j, l, n)
            tk["parts_free", j] = done
            ahead()
            flush()
            act.wait(done)
            if l == 1:
                split_v(i, n, V1[0:n, t_], ("V1", b), tk.get(("pv_done", b - 1, 1)))
            else:
                split_v(i, n, V0[0:n, t_], ("V0", b), tk.get(("pv_done", b - 1, 0)), 1.0 if t_ else mip[:, 0:1], t_ == 0)

        def g_piece(b, t_):
            c = cT[b % 2]
            n, w = ROWS[t_], T - 128 * t_
            i = bank()
            first = min(128 * t_, T - 128)
            for k in range(4):
                done = mm(R[i][0:n, first:T], c[:, k, 128 * t_:128 * t_ + n], c[:, k, first:T], k == 0, k == 3, k == 3)
            ps = R[i][0:n, 128 * t_:T]
            tk["ctx_free", b] = done
            gh, gl, o = Gh, Gl, GO[t_]
            we = w - NIP
            act.wait(done, tk.get(("y_done", b - 1)))
            hi = act.do(lambda e: e.activation(gh[0:n, o:o + n], ps[:, 0:n], ACT.Copy, scale=0.5))
            if we > n:
                hi = acopy(gh[0:n, o + n:o + we], ps[:, n:we])
            hi = acopy(g4[0:n, t_, :], ps[:, we:w])
            dve.wait(hi)
            lo = stt(gl[0:n, o:o + n], ps[:, 0:n], 0.5, gh[0:n, o:o + n].bitcast(fp32), ALU.mult, ALU.subtract)
            if we > n:
                lo = tt(dve, gl[0:n, o + n:o + we], ps[:, n:we], gh[0:n, o + n:o + we].bitcast(fp32), ALU.subtract)
            bank_free[i] = lo
            tk["G", b] = lo
            if t_ == 2:
                def rest():
                    act.wait(hi, tk.get("g4s"))
                    h = acopy(g4s[:, :, 0, :], g4[:])
                    pool.wait(h)
                    r = tt(pool, g4r[:], g4[:], g4s[:, :, 0, :], ALU.subtract)
                    pool.wait(r)
                    mid = pool.do(lambda e: e.tensor_copy(g4s[:, :, 1, :], g4r[:]))
                    pool.wait(mid)
                    low = tt(pool, g4s[:, :, 2, :], g4r[:], g4s[:, :, 1, :], ALU.subtract)

                    def last():
                        act.wait(low)
                        for u in range(3):
                            tk["W4", b] = tk["g4s"] = acopy(
                                V1[:, u, :, 49:61],
                                g4s[:, u, :, :].rearrange("p a n -> p (a n)").unsqueeze(1).to_broadcast([128, H, 12]))
                    later.append(last)
                later.append(rest)

        def q_split(b, l, rhs, token, key):
            i = bank()
            pe.wait(token, tk["wq0"] if l == 0 else tk["wq1"])
            for m, (c0, _) in enumerate(MT):
                for k, (_, n) in enumerate(CT):
                    done = mm(R[i][:, 128 * m:128 * m + 128], wq[l][0:n, k, c0:c0 + 128], rhs[0:n, k, :], k == 0, k == 2,
                              k == 2 and m == 2)
            tk[key, b] = tk[key] = done
            ps = R[i][:, 0:384].rearrange("p (m q) -> p m q", m=3)[:, :, 0:S]
            act.wait(done, tk.get("qw"))
            hi = acopy(qst[:, :, 0, :], ps, 0.25)
            dve.wait(hi, tk.get("qrem_free"))
            r = stt(qrem[:], ps, 0.25, qst[:, :, 0, :], ALU.mult, ALU.subtract)
            bank_free[i] = r
            dve.wait(r)
            mid = vcopy(qst[:, :, 1, :], qrem[:])
            pool.wait(mid)
            low = tt(pool, qst[:, :, 2, :], qrem[:], qst[:, :, 1, :], ALU.subtract)
            tk["qrem_free"] = low
            sp.wait(low)
            for m, (c0, r0) in enumerate(MT):
                tk["qw"] = d_qw[l].go(qd[l][b][:, c0 + r0:c0 + 128, :].rearrange("a r q -> r a q"), qst[r0:128, m, :, :])
            tk["qw", b, l] = tk["qw"]

        def q_stack(b, l):
            sp.wait(tk["qw", b, l], tk.get(("st_done", b - 1, l, 1)))
            for g in range(6):
                tk["Qs", b, l] = d_qr[l].go(Qs[l][D * g:D * g + D, :, :],
                                            qd[l][b, QPART[g]].rearrange("(h d) q -> d h q", d=D))

        def s_max(b, l, h0, wide):
            n, o = (3, ST) if wide else (2, PN)
            pe.wait(tk["Ks", b, l, 0 if h0 + n <= HALVES[0][1] else 1], tk["Qs", b, l], tk.get(("smax_free", wide)))
            pe.wait(*((tk.get("st_free"),) if wide else (tk.get("pv_free"), tk.get("ns_free"))))
            for u in range(n):
                done = mm(o[0:S, u, 0:T], Qs[l][0:96, h0 + u, :], Ks[l][0:96, h0 + u, 0:T], True, True, u == n - 1)
            dve.wait(done, tk.get("mn"))
            if l == 0:
                dve.do(lambda e: e.reduce_max(m0[:, h0:h0 + n], o[0:S, 0:n, 0:TEXT0], X))
                t_ = dve.do(lambda e: e.reduce_max(m0[:, H + h0:H + h0 + n], o[0:S, 0:n, TEXT0:T], X))
            else:
                dve.wait(tk.get(("fused", b - 2)))
                dve.do(lambda e: e.reduce_max(m1[:, h0:h0 + n], o[0:S, 0:n, 0:TEXT1], X))
                t_ = vcopy(sip[b % 2][:, h0:h0 + n, :], o[0:S, 0:n, TEXT1:T])
            tk["smax_free", wide] = t_
            tk["m", b, l] = t_

        def m_rows(b, l):
            n = 2 * H if l == 0 else H
            m_ = m0 if l == 0 else m1
            dve.wait(tk["m", b, l], tk.get("mT"))
            tk["mn"] = dve.do(lambda e: e.tensor_scalar(mn[:, 0:n], m_[:], -1.0, LOG_P, ALU.mult, ALU.add))
            yield
            i = bank()
            pe.wait(tk["mn"])
            done = tk["mT"] = transpose(R[i][0:n, 0:S], mn[:, 0:n], ident[0:S, 0:S], True)
            act.wait(done, tk.get("mrow"))
            acopy(mrem[0:n, :], R[i][0:n, 0:S])
            hi = acopy(ms[0:n, 0, :], R[i][0:n, 0:S])
            bank_free[i] = hi
            yield
            dve.wait(hi)
            pool.wait(hi)
            r = tt(pool, mrem[0:n, :], mrem[0:n, :], ms[0:n, 0, :], ALU.subtract)
            pool.wait(r)
            mid = pool.do(lambda e: e.tensor_copy(ms[0:n, 1, :], mrem[0:n, :]))
            pool.wait(mid)
            low = tt(pool, ms[0:n, 2, :], mrem[0:n, :], ms[0:n, 1, :], ALU.subtract)
            sp.wait(low, tk.get(("st_done", b - 1, l, 1)))
            for c in range(n // H):
                for u in range(3):
                    r0 = 96 + 3 * c + u
                    tk["mrow"] = d_m[l].go(Qs[l][r0:r0 + 1, :, :], ms[H * c:H * c + H, u, :])
            tk["mrow", b, l] = tk["mrow"]

        gcount = [0]

        def scores(b, l, g):
            rows = 102 if l == 0 else 100
            pe.wait(tk["mrow", b, l], tk.get("st_free"), tk.get(("smax_free", True)))
            for u in range(3):
                for h in range(GH):
                    done = mm(ST[:, u, S * h:S * h + S], Ks[l][0:rows, GH * g + h, 128 * u:128 * u + 128],
                              Qs[l][0:rows, GH * g + h, :], True, True, u == 2 and h == GH - 1)
            if GH * g + GH in (HALVES[0][1], HALVES[1][1]):
                tk["st_done", b, l, 0 if GH * g + GH == HALVES[0][1] else 1] = done
            n = gcount[0]
            gcount[0] += 1
            i = n % 2
            st = ST[:, :, 0:QW]
            p32v, phv = (x[:, 0:3 * QW].rearrange("p (u q) -> p u q", u=3) for x in (p32[i], ph[i]))
            act.wait(done, tk.get(("pl_done", n - 2)), tk.get(("pl_first", n - 2)), tk.get(("w2_done", n - 2)))
            t32 = act.do(lambda e: e.activation(p32v, st, ACT.Exp))
            act.wait(tk.get(("pv", n - 2)))
            th = act.do(lambda e: e.activation(phv, st, ACT.Exp))
            tk["ph", n] = th
            tk["st_free"] = th
            pool.wait(tk["ph", n], tk.get(("pv", n - 2)))
            c = QW if l == 0 else 0
            tk["pl_done", n] = tt(pool, pl[i][:, c:3 * QW], p32[i][:, c:3 * QW], ph[i][:, c:3 * QW], ALU.subtract)
            if c:
                dve.wait(tk["ph", n], tk.get(("pv", n - 2)))
                tk["pl_first", n] = tt(dve, pl[i][:, 0:c], p32[i][:, 0:c], ph[i][:, 0:c], ALU.subtract)
            return n

        def scores_r(n):
            i = n % 2
            act.wait(tk.get("y"), tk.get(("w2_done", n - 1)))
            tk["pr", n] = tk["st_free"] = act.do(lambda e: e.activation(
                pr[:].rearrange("p (u q) -> p u q", u=3), ST[:, :, 0:QW], ACT.Exp))
            dve.wait(tk["pr", n], tk.get(("ns_done", n - 2)), tk.get("n2"))
            tk["w2_done", n] = stt(w2[i][:], p32[i][:], 2.0, pr[:].bitcast(fp32), ALU.mult, ALU.subtract)

        def reduce_parts(o, x):
            return dve.do(lambda e: e.tensor_reduce(o, x, X, ALU.add))

        def pv0(b, g, n):
            i = n % 2
            pe.wait(tk["V0", b], tk["ph", n], tk["pl_done", n], tk["pl_first", n], tk.get("pv_free"), tk.get(("smax_free", False)))
            first = True
            for h in range(GH):
                hh = GH * g + h
                for c in range(2):
                    for u in ((0,) if c == 0 else (0, 1, 2)):
                        k = TEXT0 if c == 0 else 119 if u == 2 else 128
                        v = V0t[0:k, hh, :] if c == 0 else V0[0:k, u, hh, :]
                        for p_ in (ph[i], pl[i]):
                            o = QW * u + S * h
                            last = h == GH - 1 and c == 1 and u == 2 and p_ is pl[i]
                            done = mm(PV[:, 98 * h + 49 * c:98 * h + 49 * c + 49], p_[0:k, o:o + 128], v, first, last,
                                      last, True)
                            first = False
            tk["pv", n] = done
            if g == NG - 1:
                tk["pv_done", b, 0] = done
            ps = PV[0:S, 0:98 * GH].rearrange("p (c f) -> p c f", f=49)
            dve.wait(done, tk.get("acc"))
            z = dve.do(lambda e: e.reciprocal(rz[:].unsqueeze(2), ps[:, :, 48:49]))
            r = reduce_parts(acc[0][:], ps[:, :, 0:48].rearrange("p c (f d) -> p c d f", d=D))
            tk["pv_free"] = r
            dve.wait(r)
            r = tt(dve, acc[1][:], acc[0][:], rz[:].unsqueeze(2).to_broadcast([S, 2 * GH, D]), ALU.mult)
            dve.wait(r, tk.get("o0_free"), tk.get("t1_free"))
            a2 = acc[1][:].rearrange("p (h c) d -> p c h d", c=2)
            tk["o0"] = tk["acc"] = tt(dve, o0[:, 64 * g:64 * g + 64].rearrange("p (h d) -> p h d", d=D),
                                      a2[:, 0], a2[:, 1], ALU.add)

        def y_part(b, g, n):
            i = n % 2
            pe.wait(tk["G", b], tk["pr", n])
            for j in range(3):
                r_ = bank()
                nj = ROWS[j]
                mms = [(gg, u) for u in range(j + 1) for gg in (Gh, Gl)]
                for x, (gg, u) in enumerate(mms):
                    o = GO[u] + 128 * (j - u)
                    done = mm(R[r_][0:nj, 0:QW], gg[0:ROWS[u], o:o + nj], pr[0:ROWS[u], QW * u:QW * u + QW],
                              x == 0, x == len(mms) - 1, x == len(mms) - 1)
                dve.wait(done, tk["w2_done", n])
                w = w2[i][0:nj, QW * j:QW * j + QW]
                t_ = tt(dve, w, R[r_][0:nj, 0:QW], w, ALU.mult)
                bank_free[r_] = t_
                tk["prod", j] = t_
            tk["y"] = done
            if g == NG - 1:
                tk["y_done", b] = done

        def ns_part(b, g, n):
            pe.wait(tk.get("ns_free"), tk.get(("smax_free", False)))
            for j in range(3):
                pe.wait(tk["prod", j])
                tk["ns", j] = mm(NS[32 * j:32 * j + 32, 0:QW], sel[0:ROWS[j], g, :], w2[n % 2][0:ROWS[j], QW * j:QW * j + QW],
                                 g == 0, g == NG - 1, True, True)
            tk["ns_done", n] = tk["ns", 2]

        def pv1(b, g, n):
            i = n % 2
            pe.wait(tk["V1", b], tk["W4", b], tk["ph", n], tk["pl_done", n], tk.get("pv_free"),
                    tk.get(("smax_free", False)))
            first = True
            for h in range(GH):
                hh = GH * g + h
                for u in range(3):
                    for p_ in (ph[i], pl[i]):
                        o = QW * u + S * h
                        last = h == GH - 1 and u == 2 and p_ is pl[i]
                        done = mm(PV[:, 61 * h:61 * h + 61], p_[0:ROWS[u], o:o + 128], V1[0:ROWS[u], u, hh, :],
                                  first, last, last, True)
                        first = False
            tk["pv", n] = done
            if g == NG - 1:
                tk["pv_done", b, 1] = done
            ps = PV[0:S, 0:61 * GH].rearrange("p (c f) -> p c f", f=61)
            h0 = GH * g
            dve.wait(done, tk.get("num_free"), tk.get("t1_free"), tk["o0_free"], tk.get("acc"))
            vcopy(zs[:, h0:h0 + GH].unsqueeze(2), ps[:, :, 48:49])
            dve.do(lambda e: e.reciprocal(rz[:, 0:GH].unsqueeze(2), ps[:, :, 48:49]))
            reduce_parts(acc[0][:, 0:GH, :], ps[:, :, 0:48].rearrange("p c (f d) -> p c d f", d=D))
            r = reduce_parts(num[:, h0:h0 + GH, :], ps[:, :, 49:61].rearrange("p c (f d) -> p c d f", d=NIP))
            tk["pv_free"] = r
            dve.wait(r)
            tk["t1"] = tk["acc"] = tt(dve, t1[:, 64 * g:64 * g + 64].rearrange("p (h d) -> p h d", d=D), acc[0][:, 0:GH, :],
                                      rz[:, 0:GH].unsqueeze(2).to_broadcast([S, GH, D]), ALU.mult)

        def out_T(src, i_o, token):
            i = bank()
            pe.wait(token)
            for k, (c0, n) in enumerate(CT):
                done = transpose(R[i][0:n, S * k:S * k + S], src[:, c0:c0 + n], ident[0:S, 0:S], k == 2)
            act.wait(done, tk.get("oT_free"), tk.get("q1"))
            acopy(oT[:, 0:2, :], R[i][:, 0:2 * S].rearrange("p (k q) -> p k q", k=2))
            t_ = acopy(oT[0:64, 2, :], R[i][0:64, 2 * S:3 * S])
            bank_free[i] = t_
            return done, t_

        def out_mm(l, token):
            i = bank()
            pe.wait(token, tk["wo0"] if l == 0 else tk["wo1"])
            for k, n in enumerate((128, 128, 65)):
                done = mm(R[i][0:S, 0:C], oT[0:n, k, :], wo[l][0:n, k, :], k == 0, k == 2, k == 2)
            tk["oT_free"] = done
            return i, done

        def finish0(b):
            read, t_ = out_T(o0, 0, tk["o0"])
            tk["o0_free"] = read
            yield
            i, done = out_mm(0, t_)
            dve.wait(done, tk["xn", b], tk.get(("out", b - 2)))
            t_ = tt(dve, x1[b % 2][:], R[i][0:S, 0:C], xn[:], ALU.add)
            bank_free[i] = t_
            tk["x1", b] = t_
            yield
            i = bank()
            pe.wait(t_)
            for k, (c0, n) in enumerate(CT):
                done = transpose(R[i][0:n, S * k:S * k + S], x1[b % 2][:, c0:c0 + n], ident[0:S, 0:S], k == 2)
            act.wait(done, tk["oT_free"])
            acopy(x1T[:, 0:2, 0:S], R[i][:, 0:2 * S].rearrange("p (k q) -> p k q", k=2))
            t_ = acopy(x1T[0:64, 2, 0:S], R[i][0:64, 2 * S:3 * S])
            bank_free[i] = t_
            tk["x1T", b] = done
            yield
            q_split(b, 1, x1T, t_, "q1")

        def finish1(b):
            sp.wait(tk["vipd"], tk.get(("ip_mm", b - 1)))
            tk["vrep", b] = d_v.go(vbd[:], vipd[NIP * b:NIP * b + NIP, :].rearrange("(a n) c -> a n c", a=1)
                                      .to_broadcast([H, NIP, C]))
            pool.wait(tk["vrep", b])
            tk["vbd", b] = tt(pool, vbd[:], vbd[:], bmask[:], ALU.mult)
            act.wait(tk["ns", 0], tk["ns", 1], tk["ns", 2], tk.get("n2"))
            t_ = acopy(nss, NS[0:96, 0:QW])
            tk["ns_free"] = t_
            yield
            i = bank()
            pe.wait(t_)
            for h in range(GH):
                done = transpose(R[i][0:S, 96 * h:96 * h + 96], nss[:, S * h:S * h + S], ident[0:96, 0:96], h == GH - 1)
            tk["n2"] = done
            dve.wait(tk["t1"])
            z = tt(dve, zq[:], zs[:], zs[:], ALU.mult)
            dve.wait(done)
            t_ = reduce_parts(dsum[:].rearrange("p (g h) -> p g h", h=GH),
                              R[i][0:S, 0:384].rearrange("p (h j g) -> p g h j", j=3, g=32)[:, 0:NG])
            bank_free[i] = t_
            dve.wait(t_, z)
            t_ = stt(d2[:].rearrange("p (g h) -> p g h", h=GH), zq[:].rearrange("p (g h) -> p g h", h=GH), EPS2 / 2,
                     dsum[:].rearrange("p (g h) -> p g h", h=GH), ALU.mult, ALU.max)
            act.wait(t_)
            t_ = act.do(lambda e: e.activation(d2[:], d2[:], ACT.Sqrt, scale=2.0))
            yield
            dve.wait(t_)
            t_ = dve.do(lambda e: e.reciprocal(sm[0][:], d2[:]))
            dve.wait(t_)
            f0, f1 = fus
            t_ = tt(dve, f0[:], num[:], sm[0][:].unsqueeze(2).to_broadcast([S, H, NIP]), ALU.mult)
            tk["num_free"] = t_
            dve.wait(t_)
            t_ = tt(dve, f1[:], f0[:], ninv[0:S, b, :].unsqueeze(1).to_broadcast([S, H, NIP]), ALU.mult)
            dve.wait(t_)
            t_ = tt(dve, f0[:], f1[:], sip[b % 2][:], ALU.add)
            tk["fused", b] = t_
            dve.wait(t_)
            t_ = dve.do(lambda e: e.reduce_max(sm[1][:], f0[:], X))
            dve.wait(t_)
            t_ = tt(dve, f1[:], f0[:], sm[1][:].unsqueeze(2).to_broadcast([S, H, NIP]), ALU.subtract)
            act.wait(t_)
            t_ = act.do(lambda e: e.activation(f0[:], f1[:], ACT.Exp))
            yield
            dve.wait(t_)
            t_ = dve.do(lambda e: e.reduce_sum(sm[1][:], f0[:], X))
            dve.wait(t_)
            t_ = dve.do(lambda e: e.reciprocal(sm[2][:], sm[1][:]))
            dve.wait(t_)
            t_ = dve.do(lambda e: e.tensor_scalar(sm[0][:], sm[2][:], side[:, 0:1], None, ALU.mult))
            dve.wait(t_, tk.get("pr_read"))
            t_ = tt(dve, f1[:], f0[:], sm[0][:].unsqueeze(2).to_broadcast([S, H, NIP]), ALU.mult)
            yield
            i = bank()
            pe.wait(t_)
            done = transpose(R[i][0:H * NIP, 0:S], f1[:].rearrange("p h n -> p (h n)"), ident[0:S, 0:S], True)
            tk["pr_read"] = done
            act.wait(done, tk.get(("ip_mm", b - 1)))
            t_ = acopy(prT[:], R[i][0:H * NIP, 0:S])
            bank_free[i] = t_
            yield
            i = bank()
            pe.wait(t_, tk["vbd", b])
            done = mm(R[i][0:S, 0:C], prT[:], vbd[:], True, True, True)
            tk["ip_mm", b] = done
            dve.wait(done)
            t_ = tt(dve, t1[:], R[i][0:S, 0:C], t1[:], ALU.add)
            bank_free[i] = t_
            yield
            read, t_ = out_T(t1, 1, t_)
            tk["t1_free"] = read
            yield
            i, done = out_mm(1, t_)
            dve.wait(done, tk["x1T", b])
            t_ = tt(dve, x1[b % 2][:], R[i][0:S, 0:C], x1[b % 2][:], ALU.add)
            bank_free[i] = t_
            sp.wait(t_)
            tk["out", b] = d_out[b % 2].go(out[b], x1[b % 2][:])

        def values(todo):
            vs = [x for x in todo if x[1] is not None]
            at = [0]

            def parts():
                if at[0] < len(vs):
                    token_parts(vcount[0], *vs[at[0]], dve if at[0] < 2 else pool)
                    at[0] += 1
            parts()
            yield
            for b, l, t_ in todo:
                if l is None:
                    g_piece(b, t_)
                    if t_ == 2 and b + 2 < B:
                        load_ctx(b + 2, act)
                    yield
                else:
                    yield v_piece(b, l, t_, parts)

        def ahead(b):
            n = b + 1
            order = ((n, 0, 0), (b, 1, 0), (b, None, 0), (b, 1, 1), (b, None, 1), (b, 1, 2), (b, None, 2), (n, 0, 1), (n, 0, 2))
            tail = values([x for x in order if x[0] < B])
            if n < B:
                pe.wait(tk["ctx", n])
                for l, m in ((0, 0), (0, 1), (None, 0), (1, 0)):
                    yield k_piece(n, l, m)
                yield q_split(n, 0, xT, tk["xT", n], "q0")
                next(tail)
                yield k_piece(n, 1, 1)
                yield text_values(n)
            else:
                next(tail)
            yield from tail

        def take(pieces, n):
            for _ in range(n):
                next(pieces, None)

        def groups(b, l, between):
            prev = None
            for g in range(NG + 1):
                n = scores(b, l, g) if g < NG else None
                if l == 0:
                    between(g)
                if g and l == 0:
                    pv0(b, g - 1, prev)
                if g and l == 1:
                    y_part(b, g - 1, prev)
                if l == 1:
                    between(g, False)
                if n is not None and l == 1:
                    scores_r(n)
                if g and l == 1:
                    pv1(b, g - 1, prev)
                    ns_part(b, g - 1, prev)
                if l == 1:
                    between(g, True)
                prev = n

        def maxima(b, l, between):
            for h in range(0, H, 5):
                s_max(b, l, h, True)
                between()
                s_max(b, l, h + 3, False)
                between()
            return m_rows(b, l)

        clear_pads()
        load("wk0", (wk[0][:], rows("wk0")))
        load_ctx(0, sp)
        load("wkip0", (wk[1][:], rows("wkip0")))
        load("cip", (cip, rows("cip")))
        load("wkip1", (wkip, rows("wkip1")))
        load_xT(0)
        load("wq0", (wq[0][:], rows("wq0")))
        load("mip", (mip[:], a["mip"]))
        load("ident", (ident[:], a["ident"]))
        load("wvip1", (wvip, rows("wvip1")))
        load("wk1", (wk[2][:], rows("wk1")))
        load("wv0", (wv0raw, rows("wv0")))
        sp.wait(tk["pads"])
        load("ones_rows", (Ks[0][96:102, :, :], a["kones0"]), (Ks[1][96:100, :, :], a["kones1"]),
             (Qs[1][99:100, :, :], a["qone"].rearrange("(a h) q -> a h q", a=1)))
        for t_ in (act, pe, dve):
            t_.wait(tk["pool_sets"])
        pe.wait(tk["ctx", 0])
        k_piece(0, 0, 0)
        image_keys()
        k_piece(0, 0, 1)
        k_piece(0, None, 0)
        q_split(0, 0, xT, tk["xT", 0], "q0")
        sp.wait(tk["wkip_read"])
        load("wvip0", (wkip, rows("wvip0")))
        k_stack(0, 0)
        q_stack(0, 0)
        for m in range(2):
            k_piece(0, 1, m)
        load("wo0", (wo[0][:], rows("wo0")))
        load("wq1", (wq[1][:], rows("wq1")))
        load("wo1", (wo[1][:], rows("wo1")))
        load_xn(0)
        image_values()
        sp.wait(tk["vipd"])
        load_ctx(1, sp)
        sp.wait(tk["wvip_read"])
        load("wv1", (wvip, rows("wv1")))
        load("small", (sel[:], a["sel"]), (bmask[:], a["bmask"]), (side[:], a["side"]))
        dve.wait(tk["mip"], tk["v_ones"])
        tk["v_mask"] = vcopy(V0[:, 0, :, 48:49], mip[:].unsqueeze(1).to_broadcast([128, H, 1]))
        act.wait(tk["mip"])

        def weight_parts(l, token):
            raw = (wkip, wvip, wv0raw)[l]
            act.wait(token)
            t = acopy(wvh[l][:], raw)
            dve.wait(t)
            tk["wvp", l] = tt(dve, wvl[l][:], raw, wvh[l][:].bitcast(fp32), ALU.subtract)

        pe.wait(tk["ident"], tk["v_mask"], tk["oT_ones"], tk["ones_rows"])
        weight_parts(2, tk["wv0"])
        weight_parts(0, tk["wvip0"])
        ip_values = values([(0, 0, t_) for t_ in range(3)])
        next(ip_values)

        def with_maxima():
            yield text_values(0)
            yield from ip_values

        start = with_maxima()
        take(start, 3)
        rows0 = maxima(0, 0, lambda: take(start, 1))
        take(start, 99)
        flush()
        take(rows0, 9)
        weight_parts(1, tk["wv1"])
        for t_ in (pe, dve, pool):
            t_.wait(tk["small"])
        dve.wait(tk["vipd"])
        act.wait(tk["wvp", 0], tk["wvp", 1])
        rows1 = iter(())
        for b in range(B + 1):
            if b + 1 < B:
                load_xT(b + 1)
            pieces = ahead(b) if b < B else iter(())
            first, last = iter(()), iter(())

            def among0(g):
                take(rows1, 1)
                take(pieces, 1 if b + 1 < B and (b or g < 4) else 0)
                if g < 2:
                    flush()

            def among1(g, end):
                if g == 0 and b + 1 < B:
                    take(pieces, 1)
                if end or g:
                    take(first, 1)
                if end and g == 2 and b < B:
                    k_stack(b, 1, (0,))

            if not b:
                take(pieces, 2)
            if b < B:
                groups(b, 0, among0)
                first = finish0(b)
            else:
                flush()
                flush()
            take(rows1, 9)
            if not b:
                take(pieces, 2)
            if b + 1 < B:
                k_stack(b + 1, 0)
                q_stack(b + 1, 0)
            if b:
                groups(b - 1, 1, among1)
                last = finish1(b - 1)
                take(last, 1)
            else:
                k_stack(b, 1, (0,))
            take(first, 99)
            if b < B:
                k_stack(b, 1, (1,))
                q_stack(b, 1)
            if b + 1 < B:
                load_xn(b + 1)
            count = [0]
            rows0 = iter(())

            def between():
                count[0] += 1
                if count[0] > 9:
                    take(rows0, 1)
                if count[0] in (1, 2, 3, 5, 7, 9, 10):
                    take(last, 1)
                if count[0] in (2, 4, 6, 8, 11, 12, 14, 16):
                    take(pieces, 1)
            if b + 1 < B:
                rows0 = maxima(b + 1, 0, between)
                take(rows0, 1)
            if b < B:
                rows1 = maxima(b, 1, between)
                take(rows1, 1)
            take(rows0, 9)
            take(last, 99)
            take(pieces, 99)
        sp.wait(tk["out", B - 2], tk["out", B - 1])

        block = ctx.enter_context(nc.Block())

        @block.tensor
        def _(e):
            pe.run(e)

        @block.vector
        def _(e):
            dve.run(e)

        @block.scalar
        def _(e):
            act.run(e)

        @block.gpsimd
        def _(e):
            pool.run(e)

        @block.sync
        def _(e):
            sp.run(e)


def kernel(**inputs):
    import ml_dtypes
    import numpy as np
    import concourse.bacc as bacc
    from concourse.bass_utils import run_bass_kernel_spmd

    x = np.asarray(inputs["x"])
    c = np.asarray(inputs["ctx_2048"])
    g = {k: np.asarray(v) for k, v in inputs.items()}
    wk1 = g["L1_xattn_W_k"]

    def padded(w, *below):
        o = np.zeros((384, C), np.float32)
        o[0:C] = w
        for r in below:
            o[C] = r
        return o

    xT = np.zeros((384, B * S + 16), np.float32)
    xT[0:C, 0:B * S] = x.reshape(B * S, C).T
    kones0 = np.zeros((6, KW), ml_dtypes.bfloat16)
    kones0[0:3, 0:TEXT0] = 1
    kones0[3:6, TEXT0:KW] = 1
    kones1 = np.ones((4, KW), ml_dtypes.bfloat16)
    kones1[3, 0:TEXT1] = 0
    kones1[3, TEXT1:KW] = -1e30
    sel = np.zeros((128, NG, 32), np.float32)
    for i in range(NG):
        sel[:, i, i] = 1
    mip = np.ones((128, 1), np.float32)
    mip[0:TEXT0] = 0
    bmask = np.zeros((H, NIP, H, D), ml_dtypes.bfloat16)
    for h in range(H):
        bmask[h, :, h, :] = 1
    arrays = {
        "x": x,
        "xT": xT,
        "ctxT": c.transpose(0, 2, 1),
        "cip": c[:, TEXT1:].transpose(2, 0, 1).reshape(E, B * NIP),
        "wk0": np.concatenate([g["L0_xattn_Wk"].T, wk1[:, 256:]], 1),
        "wkip0": np.concatenate([g["L0_xattn_Wk_ip"].T, wk1[:, 256:]], 1), "wk1": wk1[:, 0:256],
        "wv0": g["L0_xattn_Wv"].T, "wvip0": g["L0_xattn_Wv_ip"].T, "wv1": g["L1_xattn_W_v"],
        "wq0": padded(g["L0_xattn_Wq"].T), "wo0": padded(g["L0_xattn_Wo"].T, g["L0_xattn_bo"]),
        "wq1": padded(g["L1_xattn_W_q"]), "wo1": padded(g["L1_xattn_W_out"], g["L1_xattn_b_out"]),
        "wkip1": g["L1_xattn_W_k_ip"], "wvip1": g["L1_xattn_W_v_ip"],
        "side": g["fside_S_0"].reshape(S, 1),
        "ident": np.eye(128, dtype=np.float32),
        "kones0": np.repeat(kones0[:, None], H, 1),
        "kones1": np.repeat(kones1[:, None], H, 1),
        "qone": np.ones((H, S), ml_dtypes.bfloat16),
        "sel": sel, "mip": mip,
        "bmask": bmask.reshape(H * NIP, C),
    }
    arrays = {f"in_{k}": np.ascontiguousarray(v) for k, v in arrays.items()}
    nc = bacc.Bacc("TRN2", target_bir_lowering=False, num_devices=1)
    a = {k[3:]: nc.dram_tensor(k, v.shape, mybir.dt.from_np(v.dtype), kind="ExternalInput").ap() for k, v in arrays.items()}
    out = nc.dram_tensor("out_0", (B, S, C), mybir.dt.float32, kind="ExternalOutput").ap()
    xattn_two_layers(nc, a, out)
    return run_bass_kernel_spmd(nc, [arrays], core_ids=[0]).results[0]["out_0"]
```
